# Optimizing a Trainium2 kernel written in Bass

```python
import numpy as np
import jax
import jax.numpy as jnp

def _softmax(x, axis=-1):
    return jax.nn.softmax(x, axis=axis)

def _gelu(x):
    return jax.nn.gelu(x, approximate=True)

def _silu(x):
    return jax.nn.silu(x)

def _sigmoid(x):
    return jax.nn.sigmoid(x)

def _layernorm(x, axis=-1, eps=1e-05):
    m = jnp.mean(x, axis=axis, keepdims=True)
    v = jnp.var(x, axis=axis, keepdims=True)
    return (x - m) / jnp.sqrt(v + eps)

def _scatter_add(tgt, idx, src, axis=0):
    return tgt.at[idx].add(src)

def _segment_sum(src, seg, n):
    return jax.ops.segment_sum(src, seg, n)
kernel_name = 'mk_perceiver_d1_seqx_r4_df94c9'

def setup_inputs(seed: int=0):
    np.random.seed(seed)
    _w = jnp.asarray

    def _rec_inputs():
        import jax
        import jax.numpy as jnp
        _rk = jax.random.key(seed)
        x = -0.000929 + 1 * jax.random.normal(jax.random.fold_in(_rk, 1), (1, 128, 256), jnp.float32)
        _lenS = 128 - jax.random.randint(jax.random.fold_in(_rk, 7), (1,), 0, max(1, 128 // 4) + 1, jnp.int32)
        _lenS2 = 12544 - jax.random.randint(jax.random.fold_in(_rk, 8), (1,), 0, max(1, 12544 // 4) + 1, jnp.int32)
        _ctx_1024P = jax.random.normal(jax.random.fold_in(_rk, 11), (1, 16, 256), jnp.float32)
        _ctx_1024c = jax.random.dirichlet(jax.random.fold_in(_rk, 511), 0.3 * jnp.ones((16,), jnp.float32), (1, 12544))
        _ctx_1024t = jnp.einsum('bsk,bkd->bsd', _ctx_1024c, _ctx_1024P)
        _ctx_1024t = _ctx_1024t * jax.lax.rsqrt(jnp.mean(jnp.square(_ctx_1024t)) + 1e-12) * 0.953939
        ctx_1024 = -1.52775e-05 + 0.999936 * (_ctx_1024t + 0.3 * jax.random.normal(jax.random.fold_in(_rk, 611), (1, 12544, 256), jnp.float32))
        return (x, ctx_1024)
    x, ctx_1024 = _rec_inputs()

    def _L0_xattn_setup():
        import jax, jax.numpy as jnp
        import numpy as np
        DIM = 256
        H = 16
        D = 64
        INNER = H * D
        EPS = 1e-05

        def layernorm(x, w, b):
            mu = jnp.mean(x, axis=-1, keepdims=True)
            var = jnp.var(x, axis=-1, keepdims=True)
            return (x - mu) * jax.lax.rsqrt(var + EPS) * w + b
        key = jax.random.key(seed)
        ks = jax.random.split(key, 8)
        B, N, S = (4, 64, 2048)
        s = 1.0 / np.sqrt(DIM)
        return {'latents': jax.random.normal(ks[0], (B, N, DIM), jnp.float32), 'context': jax.random.normal(ks[1], (B, S, DIM), jnp.float32), 'ln_l_w': jnp.ones((DIM,), jnp.float32), 'ln_l_b': jnp.zeros((DIM,), jnp.float32), 'ln_c_w': jnp.ones((DIM,), jnp.float32), 'ln_c_b': jnp.zeros((DIM,), jnp.float32), 'Wq': jax.random.normal(ks[2], (DIM, INNER), jnp.float32) * s, 'Wkv': jax.random.normal(ks[3], (DIM, 2 * INNER), jnp.float32) * s, 'Wo': jax.random.normal(ks[4], (INNER, DIM), jnp.float32) * (1.0 / np.sqrt(INNER)), 'bo': jnp.zeros((DIM,), jnp.float32)}
    _L0_xattn_all = _L0_xattn_setup()
    _L0_xattn_in = {k: v for k, v in _L0_xattn_all.items() if k in ('ln_l_w', 'ln_l_b', 'ln_c_w', 'ln_c_b', 'Wq', 'Wkv', 'Wo', 'bo')}
    del _L0_xattn_all

    def _L0_attn_setup():
        import jax, jax.numpy as jnp
        import numpy as np
        EMBED = 256
        HEADS = 16
        HEAD_DIM = EMBED // HEADS
        RANK = 8
        ALPHA = 16
        SCALE_LORA = ALPHA / RANK

        def _lora_linear(x, W, b, A, B):
            return x @ W.T + b + SCALE_LORA * (x @ A.T @ B.T)
        key = jax.random.key(seed)
        ks = jax.random.split(key, 17)
        d = {'x': jax.random.normal(ks[0], (2, 512, EMBED), dtype=jnp.float32)}
        names = ['q', 'k', 'v', 'o']
        i = 1
        for n in names:
            d[f'W{n}'] = jax.random.normal(ks[i], (EMBED, EMBED), dtype=jnp.float32) * 0.02
            i += 1
            d[f'b{n}'] = jnp.zeros((EMBED,), dtype=jnp.float32)
            d[f'A{n}'] = jax.random.normal(ks[i], (RANK, EMBED), dtype=jnp.float32) * 0.02
            i += 1
            d[f'B{n}'] = jax.random.normal(ks[i], (EMBED, RANK), dtype=jnp.float32) * 0.02
            i += 1
        return d
    _L0_attn_all = _L0_attn_setup()
    _L0_attn_in = {k: v for k, v in _L0_attn_all.items() if k in ('Wq', 'bq', 'Aq', 'Bq', 'Wk', 'bk', 'Ak', 'Bk', 'Wv', 'bv', 'Av', 'Bv', 'Wo', 'bo', 'Ao', 'Bo')}
    del _L0_attn_all

    def _L0_ffn_setup():
        import jax, jax.numpy as jnp
        import numpy as np
        FP8_MAX = 448.0
        FP8 = jnp.float8_e4m3fn
        key = jax.random.key(seed)
        kx, kw, kb = jax.random.split(key, 3)
        B, S, D_in, D_out = (4, 2048, 256, 256)
        x = jax.random.normal(kx, (B, S, D_in), dtype=jnp.float32)
        w = jax.random.normal(kw, (D_out, D_in), dtype=jnp.float32) * 0.02
        weight_scale = jnp.maximum(jnp.max(jnp.abs(w)), 1e-12) / FP8_MAX
        weight = (w / weight_scale).astype(FP8)
        bias = jax.random.normal(kb, (D_out,), dtype=jnp.float32) * 0.01
        return {'x': x, 'weight': weight, 'weight_scale': weight_scale, 'bias': bias}
    _L0_ffn_all = _L0_ffn_setup()
    _L0_ffn_in = {k: v for k, v in _L0_ffn_all.items() if k in ('weight', 'weight_scale', 'bias')}
    del _L0_ffn_all
    return {'x': x, 'ctx_1024': ctx_1024, 'L0_xattn_ln_l_w': _L0_xattn_in['ln_l_w'], 'L0_xattn_ln_l_b': _L0_xattn_in['ln_l_b'], 'L0_xattn_ln_c_w': _L0_xattn_in['ln_c_w'], 'L0_xattn_ln_c_b': _L0_xattn_in['ln_c_b'], 'L0_xattn_Wq': _L0_xattn_in['Wq'], 'L0_xattn_Wkv': _L0_xattn_in['Wkv'], 'L0_xattn_Wo': _L0_xattn_in['Wo'], 'L0_xattn_bo': _L0_xattn_in['bo'], 'L0_attn_Wq': _L0_attn_in['Wq'], 'L0_attn_bq': _L0_attn_in['bq'], 'L0_attn_Aq': _L0_attn_in['Aq'], 'L0_attn_Bq': _L0_attn_in['Bq'], 'L0_attn_Wk': _L0_attn_in['Wk'], 'L0_attn_bk': _L0_attn_in['bk'], 'L0_attn_Ak': _L0_attn_in['Ak'], 'L0_attn_Bk': _L0_attn_in['Bk'], 'L0_attn_Wv': _L0_attn_in['Wv'], 'L0_attn_bv': _L0_attn_in['bv'], 'L0_attn_Av': _L0_attn_in['Av'], 'L0_attn_Bv': _L0_attn_in['Bv'], 'L0_attn_Wo': _L0_attn_in['Wo'], 'L0_attn_bo': _L0_attn_in['bo'], 'L0_attn_Ao': _L0_attn_in['Ao'], 'L0_attn_Bo': _L0_attn_in['Bo'], 'L0_ffn_weight': _L0_ffn_in['weight'], 'L0_ffn_weight_scale': _L0_ffn_in['weight_scale'], 'L0_ffn_bias': _L0_ffn_in['bias']}

def reference(x, ctx_1024, L0_xattn_ln_l_w, L0_xattn_ln_l_b, L0_xattn_ln_c_w, L0_xattn_ln_c_b, L0_xattn_Wq, L0_xattn_Wkv, L0_xattn_Wo, L0_xattn_bo, L0_attn_Wq, L0_attn_bq, L0_attn_Aq, L0_attn_Bq, L0_attn_Wk, L0_attn_bk, L0_attn_Ak, L0_attn_Bk, L0_attn_Wv, L0_attn_bv, L0_attn_Av, L0_attn_Bv, L0_attn_Wo, L0_attn_bo, L0_attn_Ao, L0_attn_Bo, L0_ffn_weight, L0_ffn_weight_scale, L0_ffn_bias):
    import jax
    import jax.numpy as jnp

    def _L0_xattn_ref(latents, context, ln_l_w, ln_l_b, ln_c_w, ln_c_b, Wq, Wkv, Wo, bo):
        import jax, jax.numpy as jnp
        import numpy as np
        DIM = 256
        H = 16
        D = 64
        INNER = H * D
        EPS = 1e-05

        def layernorm(x, w, b):
            mu = jnp.mean(x, axis=-1, keepdims=True)
            var = jnp.var(x, axis=-1, keepdims=True)
            return (x - mu) * jax.lax.rsqrt(var + EPS) * w + b
        b, n, _ = latents.shape
        s = context.shape[1]
        lat = layernorm(latents, ln_l_w, ln_l_b)
        ctx = layernorm(context, ln_c_w, ln_c_b)
        q = (lat @ Wq).reshape(b, n, H, D).transpose(0, 2, 1, 3)
        kv = ctx @ Wkv
        k, v = jnp.split(kv, 2, axis=-1)
        k = k.reshape(b, s, H, D).transpose(0, 2, 1, 3)
        v = v.reshape(b, s, H, D).transpose(0, 2, 1, 3)
        scale = D ** (-0.5)
        attn = jnp.einsum('bhnd,bhsd->bhns', q, k) * scale
        attn = jnp.clip(attn, -11.0, 11.0)
        attn = jax.nn.softmax(attn, axis=-1)
        out = jnp.einsum('bhns,bhsd->bhnd', attn, v)
        out = out.transpose(0, 2, 1, 3).reshape(b, n, INNER)
        return out @ Wo + bo

    def _L0_attn_ref(x, Wq, bq, Aq, Bq, Wk, bk, Ak, Bk, Wv, bv, Av, Bv, Wo, bo, Ao, Bo):
        import jax, jax.numpy as jnp
        import numpy as np
        EMBED = 256
        HEADS = 16
        HEAD_DIM = EMBED // HEADS
        RANK = 8
        ALPHA = 16
        SCALE_LORA = ALPHA / RANK

        def _lora_linear(x, W, b, A, B):
            return x @ W.T + b + SCALE_LORA * (x @ A.T @ B.T)
        N, S, _ = x.shape
        Q = _lora_linear(x, Wq, bq, Aq, Bq).reshape(N, S, HEADS, HEAD_DIM)
        K = _lora_linear(x, Wk, bk, Ak, Bk).reshape(N, S, HEADS, HEAD_DIM)
        V = _lora_linear(x, Wv, bv, Av, Bv).reshape(N, S, HEADS, HEAD_DIM)
        energy = jnp.einsum('nqhd,nkhd->nhqk', Q, K) / jnp.sqrt(jnp.float32(HEAD_DIM))
        attn = jax.nn.softmax(energy, axis=-1)
        out = jnp.einsum('nhqk,nkhd->nqhd', attn, V).reshape(N, S, EMBED)
        return _lora_linear(out, Wo, bo, Ao, Bo)

    def _L0_ffn_ref(x, weight, weight_scale, bias):
        import jax, jax.numpy as jnp
        import numpy as np
        FP8_MAX = 448.0
        FP8 = jnp.float8_e4m3fn
        amax = jnp.max(jnp.abs(x), axis=-1, keepdims=True)
        x_scale = jnp.maximum(amax, 1e-12) / FP8_MAX
        qinput = (x / x_scale).astype(FP8)
        A = qinput.astype(x.dtype) * x_scale
        Bm = weight.astype(x.dtype) * weight_scale
        out = jnp.einsum('bsk,nk->bsn', A, Bm) + bias
        return out.astype(x.dtype)
    x = x + _L0_xattn_ref(_layernorm(x, axis=-1), ctx_1024, L0_xattn_ln_l_w, L0_xattn_ln_l_b, L0_xattn_ln_c_w, L0_xattn_ln_c_b, L0_xattn_Wq, L0_xattn_Wkv, L0_xattn_Wo, L0_xattn_bo)
    x = x + _L0_attn_ref(_layernorm(x, axis=-1), L0_attn_Wq, L0_attn_bq, L0_attn_Aq, L0_attn_Bq, L0_attn_Wk, L0_attn_bk, L0_attn_Ak, L0_attn_Bk, L0_attn_Wv, L0_attn_bv, L0_attn_Av, L0_attn_Bv, L0_attn_Wo, L0_attn_bo, L0_attn_Ao, L0_attn_Bo)
    x = x + _L0_ffn_ref(_layernorm(x, axis=-1), L0_ffn_weight, L0_ffn_weight_scale, L0_ffn_bias)
    return x

_drawn_inputs = setup_inputs


def setup_inputs(seed=0):
    import zlib

    import numpy as np

    out = dict(_drawn_inputs(seed))
    spreads = {'L0_xattn_ln_l_w': (1.0, 0.2),
     'L0_xattn_ln_l_b': (0.0, 0.481),
     'L0_xattn_ln_c_w': (1.0, 0.2),
     'L0_xattn_ln_c_b': (0.0, 0.1),
     'L0_xattn_bo': (0.0, 0.1),
     'L0_attn_bq': (0.0, 0.8),
     'L0_attn_bk': (0.0, 2.0),
     'L0_attn_bv': (0.0, 0.291),
     'L0_attn_bo': (0.0, 0.41)}
    factors = {'L0_attn_Wq': 8.0,
     'L0_attn_Aq': 8.0,
     'L0_attn_Bq': 8.0,
     'L0_attn_Wk': 8.0,
     'L0_attn_Ak': 8.0,
     'L0_attn_Bk': 8.0,
     'L0_attn_Av': 8.0,
     'L0_attn_Bv': 7.918,
     'L0_attn_Ao': 8.0,
     'L0_attn_Bo': 8.0,
     'L0_ffn_bias': 27.822}
    for name, (base, spread) in spreads.items():
        noise = np.random.default_rng([zlib.crc32(name.encode()), seed]).standard_normal(out[name].shape)
        drawn = base * np.exp(spread * noise) if base else spread * noise
        out[name] = jnp.asarray(drawn.astype(out[name].dtype))
    for name, factor in factors.items():
        out[name] = (out[name] * factor).astype(out[name].dtype)
    return out
```

```python
from contextlib import ExitStack

import numpy as np
import concourse.bass as bass
from concourse import mybir

ALU = mybir.AluOpType
ACT = mybir.ActivationFunctionType
AX_X = mybir.AxisListType.X
F32 = mybir.dt.float32
F32R = mybir.dt.float32r
BF16 = mybir.dt.bfloat16
U8 = mybir.dt.uint8
U16 = mybir.dt.uint16
I32 = mybir.dt.int32
FP16 = mybir.dt.float16

P = 128
EPS = 1e-5
FP8_MAX = 448.0
LORA_SCALE = 2.0


def perceiver_layer(
    nc, x, ctx, ln_l_w, ln_l_b, ln_c_w, ln_c_b, Wq, Wkv, Wo, bo,
    aWq, abq, aAq, aBq, aWk, abk, aAk, aBk, aWv, abv, aAv, aBv, aWo, abo, aAo, aBo,
    f_weight, f_scale, f_bias, out,
):
    _, N, D = x.shape
    S = ctx.shape[1]
    INNER = Wq.shape[1]
    H = 16
    DH = INNER // H
    KD = D // P
    MI = INNER // P
    TILES = S // P
    PAIRS = TILES // 2
    PASSES = 2
    HP = H // PASSES
    CH = 2
    CW = HP * P // CH
    HC = HP // CH
    ALL = PASSES * TILES
    SCALE = DH ** -0.5
    EXP_LO, EXP_HI = (float(np.float32(np.exp(np.float64(s)))) for s in (-11.0, 11.0))
    AH = 16
    AD = D // AH
    R = aAq.shape[0]
    HT = P // AD
    VW = DH + 1
    HB = 512 // VW
    assert N == P and S == TILES * P and TILES == 2 * PAIRS and D == 2 * P

    with ExitStack() as stack:
        def sb(name, shape, dt=F32):
            return stack.enter_context(nc.sbuf_tensor(name, shape, dt))

        def sem(name):
            return stack.enter_context(nc.semaphore(name))

        bank = [stack.enter_context(nc.psum_tensor(f"bank{n}", [P, 512], F32)) for n in range(8)]
        acc = [[bank[k * CH + c] for c in range(CH)] for k in range(KD)]
        sc_bank = bank[4:6]
        tr_bank = bank[6:8]

        ident = sb("ident", [P, P])
        identb = sb("identb", [P, P], BF16)
        ones = sb("ones", [P, D])
        ones_row = ones[0:1, 0:P]
        last_row = sb("last_row", [P, 1])
        neg_half = sb("neg_half", [P, 1])
        head_mask = sb("head_mask", [P, HT])

        x_sb = sb("x_sb", [P, D])
        lat_w, lat_b = sb("lat_w", [P, KD]), sb("lat_b", [P, KD])
        ctx_w, ctx_b = sb("ctx_w", [P, KD]), sb("ctx_b", [P, KD])
        wq = sb("wq", [P, KD, INNER])
        wk = sb("wk", [P, KD, INNER])
        wv = sb("wv", [P, KD, INNER])
        wo = sb("wo", [P, MI, D])
        bo_row = sb("bo_row", [1, D])
        aw = [sb(f"aw{n}", [P, KD, D]) for n in range(4)]
        aa = [sb(f"aa{n}", [R, D]) for n in range(4)]
        ab = [sb(f"ab{n}", [P, KD, R]) for n in range(4)]
        abq_col, abk_col = sb("abq_col", [P, KD]), sb("abk_col", [P, KD])
        abv_row, abo_row = sb("abv_row", [1, D]), sb("abo_row", [1, D])
        f_bytes = sb("f_bytes", [P, KD, D], U8)
        f_ws = sb("f_ws", [P, 1])
        f_b = sb("f_b", [P, D])

        xn = sb("xn", [P, D])
        lat = sb("lat", [P, D])
        stats = sb("stats", [P, 6])
        mv = sb("mv", [P, 2])
        veps = sb("veps", [P, 1])
        rstd = sb("rstd", [P, 1])
        latT = sb("latT", [P, KD, P])
        qTbd = sb("qTbd", [P, MI, 2, P])
        wkT = sb("wkT", [P, MI, D])
        qk_hi = sb("qk_hi", [P, KD, H * P], F32R)
        qk_lo = sb("qk_lo", [P, KD, H * P], F32R)

        x_tile = [sb(f"x_tile{b}", [P, D]) for b in range(2)]
        c_stats = [sb(f"c_stats{b}", [P, 6]) for b in range(2)]
        c_mv = [sb(f"c_mv{b}", [P, 2]) for b in range(2)]
        c_veps = [sb(f"c_veps{b}", [P, 1]) for b in range(2)]
        c_rstd = [sb(f"c_rstd{b}", [P, 1]) for b in range(2)]
        z = [sb(f"z{b}", [P, D]) for b in range(2)]
        z_hi = [sb(f"z_hi{b}", [P, D], F32R) for b in range(2)]
        z_lo = [sb(f"z_lo{b}", [P, D], F32R) for b in range(2)]
        cT = [sb(f"cT{b}", [P, KD, P]) for b in range(2)]
        cT_hi = [sb(f"cT_hi{b}", [P, KD, P], F32R) for b in range(2)]
        cT_lo = [sb(f"cT_lo{b}", [P, KD, P], F32R) for b in range(2)]
        ex = [sb(f"ex{c}", [P, CW]) for c in range(CH)]
        p_hi = [[sb(f"p_hi{b}{c}", [P, CW], F32R) for c in range(CH)] for b in range(2)]
        p_lo = [[sb(f"p_lo{b}{c}", [P, CW], F32R) for c in range(CH)] for b in range(2)]
        sums = sb("sums", [P, KD, H * P])

        foldT = sb("foldT", [P, KD, D])
        neg_w_last = sb("neg_w_last", [P, 1])
        wvE = sb("wvE", [P, KD, H, VW])
        recip = sb("recip", [P, H])
        att = wk[:, 0, :].rearrange("p (h d) -> p h d", h=H)
        attT = wk[:, 1, :].rearrange("p (m q) -> p m q", m=MI)
        x1 = sb("x1", [P, D])
        abT = sb("abT", [R, 4, D])
        awE = [sb(f"awE{n}", [P, KD, D]) for n in range(4)]
        hn = sb("hn", [P, D])
        hT = sb("hT", [P, KD, P])
        aqT = sb("aqT", [P, KD, P])
        akT = wkT[:, :, :].rearrange("p m d -> p (m d)").rearrange("p (k h t) -> p k h t", k=KD, h=HT)
        av = sb("av", [P, AH, AD + 1])
        a_max = sb("a_max", [P, AH])
        a_p = wq[:, :, :].rearrange("p k n -> p (k n)").rearrange("p (h t) -> p h t", h=AH)
        a_pT = qTbd[:, :, :, :].rearrange("p m a q -> p (m a) q")
        a_recip = sb("a_recip", [P, AH])
        ao = sb("ao", [P, AH, AD])
        aoT = sb("aoT", [P, KD, P])
        x2 = sb("x2", [P, D])
        x2b = sb("x2b", [P, D])
        fn = sb("fn", [P, D])
        amax = sb("amax", [P, 1])
        f_xs = sb("f_xs", [P, 1])
        f_inv = sb("f_inv", [P, 1])
        f_row_scale = sb("f_row_scale", [P, 1])
        fv = sb("fv", [P, D])
        f_pow = sb("f_pow", [P, D])
        f_magic = sb("f_magic", [P, D])
        f_sum = sb("f_sum", [P, D])
        f_q = sb("f_q", [P, D], BF16)
        f_qT = sb("f_qT", [P, KD, P], BF16)
        f_u = sb("f_u", [P, KD, D], U16)
        f_mag = sb("f_mag", [P, KD, D], U16)
        f_sgn = sb("f_sgn", [P, KD, D], U16)
        f_h = sb("f_h", [P, KD, D], U16)
        f_w = sb("f_w", [P, KD, D], BF16)
        f_wT = sb("f_wT", [P, KD, D], BF16)
        y = sb("y", [P, D])

        s_x = sem("x_loaded")
        s_cols = sem("cols_loaded")
        s_wq = sem("wq_loaded")
        s_wk = sem("wk_loaded")
        s_late = sem("late_weights_loaded")
        s_const = sem("pool_constants_ready")
        s_dstep = sem("dve_step_done")
        s_pstep = sem("pool_step_done")
        s_var = sem("variance_ready")
        s_rstd = sem("rstd_ready")
        s_latn = sem("lat_normalised")
        s_latTp = sem("lat_transposed")
        s_latT = sem("latT_ready")
        s_wkTp = sem("wk_transposed")
        s_wkT = sem("wkT_ready")
        s_qTp = sem("qT_computed")
        s_qTtop = sem("qT_upper_heads_ready")
        s_qTbot = sem("qT_lower_heads_ready")
        s_qkp = sem("qk_computed")
        s_qkhi = sem("qk_hi_ready")
        s_qklo = sem("qk_lo_ready")
        s_tile = [sem(f"ctx_tile{b}_loaded") for b in range(2)]
        s_cvar = sem("ctx_variance_ready")
        s_crstd = sem("ctx_rstd_ready")
        s_z = sem("z_ready")
        s_zsplit = sem("z_split_ready")
        s_tr = sem("z_transposed")
        s_cT = sem("cT_ready")
        s_cTsplit = sem("cT_split_ready")
        s_scores = sem("scores_ready")
        s_exp = sem("exp_ready")
        s_psplit = sem("probs_split_ready")
        s_pv = sem("pv_done")
        s_save = [sem(f"sums_saved{c}") for c in range(CH)]
        s_foldT = sem("foldT_ready")
        s_wvp = sem("wvE_computed")
        s_wvE = sem("wvE_ready")
        s_zhi = sem("z_hi_ready")
        s_cst = sem("ctx_stats_ready")
        s_cag = sem("ctx_mean_var_ready")
        s_cth = sem("cT_hi_ready")
        s_phi = sem("probs_hi_ready")
        s_clip = sem("probs_clipped")
        s_heads = sem("head_outputs_computed")
        s_abTp = sem("loraB_transposed")
        s_abT = sem("loraB_ready")
        s_awp = sem("attn_weights_computed")
        s_awE = sem("attn_weights_ready")
        s_recip = sem("denominators_inverted")
        s_att = sem("head_outputs_normalised")
        s_attTp = sem("head_outputs_transposed")
        s_attT0 = sem("attT_heads_0_7_ready")
        s_attT1 = sem("attT_heads_8_15_ready")
        s_xattn = sem("cross_attention_computed")
        s_hn = sem("h_normalised")
        s_hTp = sem("h_transposed")
        s_hT = sem("hT_ready")
        s_aqkp = sem("self_qk_computed")
        s_avp = sem("self_v_computed")
        s_aqT = sem("self_qT_ready")
        s_akT = sem("self_kT_ready")
        s_av = sem("self_v_ready")
        s_ascore = sem("self_scores_computed")
        s_amax = sem("self_max_ready")
        s_ashift = sem("self_scores_shifted")
        s_aexp = sem("self_exp_ready")
        s_apTp = sem("self_probs_transposed")
        s_apT_even = sem("self_probsT_even_banks_ready")
        s_apT_odd = sem("self_probsT_odd_banks_ready")
        s_apv = sem("self_outputs_computed")
        s_ao = sem("self_outputs_normalised")
        s_aoTp = sem("self_outputs_transposed")
        s_aoT = sem("self_outputsT_ready")
        s_attn = sem("self_attention_computed")
        s_fw = sem("fp8_weights_decoded")
        s_fwTp = sem("fp8_weights_transposed")
        s_fwT = sem("fp8_weightsT_ready")
        s_fq = sem("fp8_rows_rounded")
        s_fqTp = sem("fp8_rows_transposed")
        s_fqT = sem("fp8_rowsT_ready")
        s_ffn = sem("fp8_linear_computed")
        s_y = sem("y_ready")
        s_out = sem("out_stored")

        LATE = 16 * (3 + 4 * 3 + 4 + 3)
        COLS = 16 * 4

        def col(v):
            return v.rearrange("(k p) -> p k", p=P)

        def row(v):
            return v.rearrange("(a d) -> a d", a=1)

        def rows(w):
            return w.rearrange("(k p) n -> p k n", p=P)

        x_rows = x.rearrange("a n d -> (a n) d")
        out_rows = out.rearrange("a n d -> (a n) d")
        ctx_rows = ctx.rearrange("a s d -> (a s) d")
        wkv = rows(Wkv)

        block = stack.enter_context(nc.Block())

        def passes(eng, pair, tail_pairs=1):
            for p in range(PASSES):
                pair(p, 0)
                with eng.Fori(1, PAIRS - tail_pairs) as i:
                    pair(p, i)
                for i in range(PAIRS - tail_pairs, PAIRS):
                    pair(p, i)

        @block.sync
        def _(sp):
            sp.dma_start(x_sb[:, :], x_rows).then_inc(s_x, 16)
            sp.dma_start(wq[:, :, :], rows(Wq)).then_inc(s_wq, 16)
            for b in range(2):
                sp.dma_start(x_tile[b][:, :], ctx_rows[b * P:(b + 1) * P, :]).then_inc(s_tile[b], 16)
            sp.dma_start(wk[:, :, :], wkv[:, :, 0:INNER]).then_inc(s_wk, 16)

            def load(p, i):
                for b in range(2):
                    sp.wait_ge(s_z, 2 * (p * PAIRS + i) + b - 1)
                    sp.dma_start(x_tile[b][:, :], ctx_rows[bass.ds((2 * i + b) * P, P), :]).then_inc(s_tile[b], 16)

            for p in range(PASSES):
                if p > 0:
                    load(p, 0)
                with sp.Fori(1, PAIRS) as i:
                    load(p, i)

            sp.wait_ge(s_out, 16)

        @block.gpsimd
        def _(pool):
            steps = [0]

            def const_step(ins):
                steps[0] += 1
                ins.then_inc(s_pstep, 1)
                pool.wait_ge(s_pstep, steps[0])

            const_step(pool.memset(ident[:, :], 0.0))
            pool.affine_select(out=ident[:, :], in_=ident[:, :], compare_op=ALU.not_equal, fill=1.0, base=0,
                               pattern=[[-1, P]], channel_multiplier=1).then_inc(s_const, 1)
            pool.memset(neg_half[:, :], -0.5).then_inc(s_const, 1)
            pool.memset(qTbd[:, :, :, :], 0.0).then_inc(s_const, 1)

            def inv_sqrt(n):
                pool.wait_ge(s_var, n)
                pool.tensor_tensor(rstd[:, :], veps[:, :], neg_half[:, :], ALU.pow).then_inc(s_rstd, 1)

            def ctx_rstd(g, b):
                pool.wait_ge(s_cvar, g + 1)
                pool.tensor_tensor(c_rstd[b][:, :], c_veps[b][:, :], neg_half[:, :], ALU.pow).then_inc(s_crstd, 1)

            const_step(pool.memset(ones[:, :], 1.0))
            inv_sqrt(1)
            inv_sqrt(2)
            for b in range(2):
                const_step(pool.memset(z_hi[b][:, D - 1:D].bitcast(F32), 1.0))
                const_step(pool.memset(z_lo[b][:, D - 1:D].bitcast(F32), 0.0))
            const_step(pool.memset(last_row[:, :], 0.0))
            pool.affine_select(out=last_row[:, :], in_=last_row[:, :], compare_op=ALU.not_equal, fill=1.0,
                               base=-(P - 1), pattern=[[0, 1]], channel_multiplier=1).then_inc(s_const, 1)
            const_step(pool.memset(head_mask[:, :], 1.0))
            const_step(pool.affine_select(out=head_mask[:, :], in_=head_mask[:, :], compare_op=ALU.is_ge, fill=0.0,
                                          base=0, pattern=[[-AD, HT]], channel_multiplier=1))
            pool.affine_select(out=head_mask[:, :], in_=head_mask[:, :], compare_op=ALU.is_ge, fill=0.0,
                               base=AD - 1, pattern=[[AD, HT]], channel_multiplier=-1).then_inc(s_const, 1)
            pool.memset(av[:, :, AD:AD + 1], 1.0).then_inc(s_const, 1)
            pool.memset(foldT[:, 0, P:D], 0.0).then_inc(s_const, 1)

            def split_z(g, b, first=False):
                pool.wait_ge(s_z, g + 1)
                if not first:
                    pool.wait_ge(s_pv, CH * (g - 1))
                pool.tensor_tensor(z_hi[b][:, 0:D - 1], z[b][:, 0:D - 1], ones[:, 0:D - 1], ALU.mult).then_inc(s_zhi, 1)
                pool.wait_ge(s_zhi, g + 1)
                pool.tensor_tensor(z_lo[b][:, 0:D - 1], z[b][:, 0:D - 1], z_hi[b][:, 0:D - 1].bitcast(F32),
                                   ALU.subtract).then_inc(s_zsplit, 1)

            for g in range(3):
                ctx_rstd(g, g % 2)
            split_z(0, 0, first=True)

            def pair(p, i):
                for b in range(2):
                    g = 2 * (p * PAIRS + i) + b
                    last = p == PASSES - 1 and isinstance(i, int)
                    if not (last and g + 1 >= ALL):
                        split_z(g + 1, 1 - b, first=(p == 0 and isinstance(i, int) and g == 0))
                    if not (last and g + 3 >= ALL):
                        ctx_rstd(g + 3, 1 - b)

            passes(pool, pair, 2)
            for n in range(2):
                inv_sqrt(3 + n)

        @block.tensor
        def _(pe):
            def mm3(dst, hi, lo, mhi, mlo, start, stop):
                pe.matmul(dst, hi, mhi, start=start, stop=False)
                pe.matmul(dst, hi, mlo, start=False, stop=False)
                return pe.matmul(dst, lo, mhi, start=False, stop=stop)

            def transpose_z(g, b, first=False):
                pe.wait_ge(s_z, g + 1)
                if not first:
                    pe.wait_ge(s_cT, g - 1)
                for k in range(KD):
                    ins = pe.transpose(tr_bank[b][:, k * P:(k + 1) * P], z[b][:, k * P:(k + 1) * P], ident[:, :])
                ins.then_inc(s_tr, 1)

            def scores(p, g, b, c, first=False):
                pe.wait_ge(s_cTsplit, g + 1)
                if not first:
                    pe.wait_ge(s_exp, CH * (g - 1) + c + 1)
                cols = slice(p * HP * P + c * CW, p * HP * P + (c + 1) * CW)
                for k in range(KD):
                    ins = mm3(sc_bank[c][:, :], cT_hi[b][:, k, :], cT_lo[b][:, k, :], qk_hi[:, k, cols],
                              qk_lo[:, k, cols], k == 0, k == KD - 1)
                ins.then_inc(s_scores, 1)

            def weighted_sum(g, b, c, start, stop, saved=0):
                pe.wait_ge(s_psplit, CH * g + c + 1)
                if c == 0:
                    pe.wait_ge(s_zsplit, g + 1)
                if saved:
                    pe.wait_ge(s_save[c], saved)
                for k in range(KD):
                    ks = slice(k * P, (k + 1) * P)
                    ins = mm3(acc[k][c][:, :], z_hi[b][:, ks], z_lo[b][:, ks], p_hi[b][c][:, :], p_lo[b][c][:, :],
                              start, stop)
                ins.then_inc(s_pv, 1)

            pe.wait_ge(s_const, 1)
            pe.wait_ge(s_latn, 1)
            for k in range(KD):
                ins = pe.transpose(bank[0][:, k * P:(k + 1) * P], lat[:, k * P:(k + 1) * P], ident[:, :])
            ins.then_inc(s_latTp, 1)
            transpose_z(0, 0, first=True)
            transpose_z(1, 1, first=True)
            pe.wait_ge(s_wq, 16)
            pe.wait_ge(s_latT, KD)
            for m in range(MI):
                for k in range(KD):
                    ins = pe.matmul(bank[4 + m // 4][:, (m % 4) * P:(m % 4 + 1) * P], wq[:, k, m * P:(m + 1) * P],
                                    latT[:, k, :], start=(k == 0), stop=(k == KD - 1))
                if m % 4 == 3:
                    ins.then_inc(s_qTp, 1)
            pe.wait_ge(s_wk, 16)
            for m in range(MI):
                for k in range(KD):
                    ins = pe.transpose(bank[m // 2][:, (m % 2) * D + k * P:(m % 2) * D + (k + 1) * P],
                                       wk[:, k, m * P:(m + 1) * P], ident[:, :])
                if m % 2 == 1:
                    ins.then_inc(s_wkTp, 1)
            order = [4, 5, 0, 1, 2, 3, 4, 5]
            for n in range(MI // 2 * KD):
                mm, k = n // KD, n % KD
                pe.wait_ge(s_wkT, mm + 1)
                if mm % 2 == 0:
                    pe.wait_ge(s_qTtop, mm // 2 + 1)
                    pe.wait_ge(s_qTbot, mm // 2 + 1)
                if n == 0:
                    pe.wait_ge(s_qTtop, 2)
                    pe.wait_ge(s_qTbot, 2)
                if n == 2:
                    pe.wait_ge(s_wkT, 4)
                if n >= 6:
                    pe.wait_ge(s_qklo, n - 5)
                    pe.wait_ge(s_qkhi, n - 5)
                for j in range(2):
                    m = 2 * mm + j
                    ins = pe.matmul(bank[order[n]][:, j * 2 * P:(j + 1) * 2 * P], wkT[:, m, k * P:(k + 1) * P],
                                    qTbd[:, m, :, :].rearrange("p a q -> p (a q)"), start=True, stop=True)
                ins.then_inc(s_qkp, 1)

            pe.wait_ge(s_qkhi, 8)
            pe.wait_ge(s_qklo, 8)
            for c in range(CH):
                scores(0, 0, 0, c, first=True)

            def pair(p, i):
                for b in range(2):
                    g = 2 * (p * PAIRS + i) + b
                    static = isinstance(i, int)
                    next_p = p + 1 if static and i == PAIRS - 1 and b == 1 else p
                    first = static and i == 0 and b == 0
                    last = static and i == PAIRS - 1 and b == 1
                    ended = static and p == PASSES - 1
                    for c in range(CH):
                        if not (ended and g + 1 >= ALL):
                            scores(next_p, g + 1, 1 - b, c)
                        if c == 0 and not (ended and g + 2 >= ALL):
                            transpose_z(g + 2, b)
                        weighted_sum(g, b, c, first, last, saved=p * KD if first else 0)

            passes(pe, pair, 1)

            pe.wait_ge(s_late, LATE)
            pe.wait_ge(s_foldT, 1)
            pe.wait_ge(s_exp, CH * ALL)
            pe.wait_ge(s_cT, ALL)
            for n in range(4):
                kd, half = n // 2, n % 2
                for k in range(KD):
                    ins = pe.matmul(bank[4 + n][:, :], foldT[:, k, kd * P:(kd + 1) * P],
                                    wv[:, k, half * 512:(half + 1) * 512], start=(k == 0), stop=(k == KD - 1))
                ins.then_inc(s_wvp, 1)
            pe.wait_ge(s_wvE, 5)
            for c in range(CH):
                pe.wait_ge(s_save[c], PASSES * KD)
            for h in range(H):
                o = bank[h // HB][:, (h % HB) * VW:(h % HB + 1) * VW]
                for k in range(KD):
                    ins = pe.matmul(o, sums[:, k, h * P:(h + 1) * P], wvE[:, k, h, :], start=(k == 0),
                                    stop=(k == KD - 1))
            ins.then_inc(s_heads, 1)
            for n in range(4):
                for m in range(KD):
                    ins = pe.matmul(bank[4 + n // 2][0:R, (n % 2) * D + m * P:(n % 2) * D + (m + 1) * P],
                                    ab[n][:, m, :], ident[:, :], start=True, stop=True)
            ins.then_inc(s_abTp, 1)
            pe.wait_ge(s_abT, 2)
            for n in range(4):
                for k in range(KD):
                    for m in range(KD):
                        dst = bank[4 + n][:, k * D + m * P:k * D + (m + 1) * P]
                        pe.matmul(dst, aw[n][:, m, k * P:(k + 1) * P], ident[:, :], start=True, stop=False)
                        ins = pe.matmul(dst, aa[n][:, k * P:(k + 1) * P], abT[:, n, m * P:(m + 1) * P],
                                        start=False, stop=True)
                ins.then_inc(s_awp, 1)
            pe.wait_ge(s_att, 3)
            pe.wait_ge(s_awE, 2)
            for m in range(MI):
                ins = pe.transpose(bank[4 + m // 4][:, (m % 4) * P:(m % 4 + 1) * P],
                                   att[:, :, :].rearrange("p h d -> p (h d)")[:, m * P:(m + 1) * P], ident[:, :])
                if m % 4 == 3:
                    ins.then_inc(s_attTp, 1)
            pe.wait_ge(s_attT0, 1)
            pe.wait_ge(s_attT1, 1)
            for m in range(MI):
                pe.matmul(bank[0][:, 0:D], attT[:, m, :], wo[:, m, :], start=(m == 0), stop=False)
            pe.matmul(bank[0][:, 0:D], ones_row[:, :], bo_row[:, :], start=False, stop=True).then_inc(s_xattn, 1)
            pe.wait_ge(s_hn, 1)
            for k in range(KD):
                ins = pe.transpose(bank[1][:, k * P:(k + 1) * P], hn[:, k * P:(k + 1) * P], ident[:, :])
            ins.then_inc(s_hTp, 1)
            pe.wait_ge(s_hT, 1)
            pe.wait_ge(s_awE, 4)
            for n in range(2):
                for m in range(KD):
                    for k in range(KD):
                        ins = pe.matmul(bank[2 + n][:, m * P:(m + 1) * P], awE[n][:, k, m * P:(m + 1) * P],
                                        hT[:, k, :], start=(k == 0), stop=(k == KD - 1))
                ins.then_inc(s_aqkp, 1)
            for k in range(KD):
                pe.matmul(bank[1][:, 0:D], hT[:, k, :], awE[2][:, k, :], start=(k == 0), stop=False)
            pe.matmul(bank[1][:, 0:D], ones_row[:, :], abv_row[:, :], start=False, stop=True).then_inc(s_avp, 1)
            pe.wait_ge(s_aqT, 1)
            for n in range(4):
                m, half = n // 2, n % 2
                pe.wait_ge(s_akT, m + 1)
                pe.matmul(bank[4 + n][:, :], aqT[:, m, :],
                          akT[:, m, 4 * half:4 * half + 4, :].rearrange("p h t -> p (h t)"),
                          start=True, stop=True).then_inc(s_ascore, 1)
            pe.wait_ge(s_av, 1)
            for n in range(4):
                pe.wait_ge(s_aexp, n + 1)
                for j in range(4):
                    ins = pe.transpose(bank[n][:, j * P:(j + 1) * P], a_p[:, 4 * n + j, :], ident[:, :])
                ins.then_inc(s_apTp, 1)
            pe.wait_ge(s_apT_even, 2)
            pe.wait_ge(s_apT_odd, 2)
            for h in range(AH):
                ins = pe.matmul(bank[4][:, h * (AD + 1):(h + 1) * (AD + 1)], a_pT[:, h, :], av[:, h, :],
                                start=True, stop=True)
            ins.then_inc(s_apv, 1)
            pe.wait_ge(s_fw, 1)
            fw_bank = bank[7][:, :].bitcast(BF16)
            for m in range(KD):
                for k in range(KD):
                    ins = pe.transpose(fw_bank[:, k * D + m * P:k * D + (m + 1) * P], f_w[:, m, k * P:(k + 1) * P],
                                       identb[:, :])
            ins.then_inc(s_fwTp, 1)
            pe.wait_ge(s_ao, 1)
            for k in range(KD):
                ins = pe.transpose(bank[5][:, k * P:(k + 1) * P],
                                   ao[:, :, :].rearrange("p h d -> p (h d)")[:, k * P:(k + 1) * P], ident[:, :])
            ins.then_inc(s_aoTp, 1)
            pe.wait_ge(s_aoT, 1)
            for k in range(KD):
                pe.matmul(bank[6][:, 0:D], aoT[:, k, :], awE[3][:, k, :], start=(k == 0), stop=False)
            pe.matmul(bank[6][:, 0:D], ones_row[:, :], abo_row[:, :], start=False, stop=True).then_inc(s_attn, 1)
            pe.wait_ge(s_fq, 1)
            fq_bank = bank[0][:, :].bitcast(BF16)
            for k in range(KD):
                ins = pe.transpose(fq_bank[:, k * P:(k + 1) * P], f_q[:, k * P:(k + 1) * P], identb[:, :])
            ins.then_inc(s_fqTp, 1)
            pe.wait_ge(s_fqT, 1)
            pe.wait_ge(s_fwT, 1)
            for k in range(KD):
                ins = pe.matmul(bank[1][:, 0:D], f_qT[:, k, :], f_wT[:, k, :], start=(k == 0), stop=(k == KD - 1))
            ins.then_inc(s_ffn, 1)

        @block.scalar
        def _(act):
            for dst, src in ((lat_w, ln_l_w), (lat_b, ln_l_b), (ctx_w, ln_c_w), (ctx_b, ln_c_b)):
                act.dma_start(dst[:, :], col(src), allow_slow_non_contiguous=True).then_inc(s_cols, 16)

            def late(dst, src):
                act.dma_start(dst, src, allow_slow_non_contiguous=True).then_inc(s_late, 16)

            def load_late():
                late(wv[:, :, :], wkv[:, :, INNER:2 * INNER])
                late(wo[:, :, :], rows(Wo))
                late(bo_row[:, :], row(bo))
                for n, (w, a, b_) in enumerate(((aWq, aAq, aBq), (aWk, aAk, aBk), (aWv, aAv, aBv), (aWo, aAo, aBo))):
                    late(aw[n][:, :, :], rows(w))
                    late(aa[n][:, :], a)
                    late(ab[n][:, :, :], rows(b_))
                late(abq_col[:, :], col(abq))
                late(abk_col[:, :], col(abk))
                late(abv_row[:, :], row(abv))
                late(abo_row[:, :], row(abo))
                late(f_bytes[:, :, :], rows(f_weight.bitcast(U8)))
                late(f_ws[:, :], scale_bc)
                late(f_b[:, :], bias_bc)

            scale_bc = bass.AP(f_scale.tensor, 0, [[0, P], [1, 1]])
            bias_bc = bass.AP(f_bias.tensor, 0, [[0, P], [1, D]])

            act.wait_ge(s_cols, COLS)
            act.wait_ge(s_latTp, 1)
            for k in range(KD):
                act.activation(latT[:, k, :], bank[0][:, k * P:(k + 1) * P], ACT.Identity, bias=lat_b[:, k:k + 1],
                               scale=lat_w[:, k:k + 1]).then_inc(s_latT, 1)

            def evac_cT(g, b, first=False):
                act.wait_ge(s_tr, g + 1)
                if not first:
                    act.wait_ge(s_cTsplit, g - 1)
                for k in range(KD):
                    ins = act.activation(cT[b][:, k, :], tr_bank[b][:, k * P:(k + 1) * P], ACT.Identity,
                                         bias=ctx_b[:, k:k + 1], scale=ctx_w[:, k:k + 1])
                ins.then_inc(s_cT, 1)

            def exps(g, c, first=False):
                act.wait_ge(s_scores, CH * g + c + 1)
                if not first:
                    act.wait_ge(s_psplit, CH * (g - 1) + c + 1)
                act.activation(ex[c][:, :], sc_bank[c][:, :], ACT.Exp, scale=SCALE).then_inc(s_exp, 1)

            evac_cT(0, 0, first=True)
            evac_cT(1, 1, first=True)
            act.wait_ge(s_const, 3)
            for n in range(2):
                act.wait_ge(s_qTp, n + 1)
                act.copy(qTbd[0:DH, 4 * n:4 * n + 4, 0, :],
                         bank[4 + n][0:DH, :].rearrange("p (m q) -> p m q", m=4)).then_inc(s_qTtop, 1)
            for n in range(0, 4, 2):
                act.wait_ge(s_wkTp, n + 1)
                if n:
                    act.wait_ge(s_wkT, n)
                act.copy(wkT[:, 2 * n:2 * n + 2, :], bank[n][:, :].rearrange("p (m d) -> p m d", m=2))\
                   .then_inc(s_wkT, 1)
            order = [4, 5, 0, 1, 2, 3, 4, 5]
            for n in range(8):
                mm, k = n // KD, n % KD
                act.wait_ge(s_qkp, n + 1)
                act.copy(qk_hi[:, k, mm * 512:(mm + 1) * 512], bank[order[n]][:, :]).then_inc(s_qkhi, 1)
            load_late()
            exps(0, 0, first=True)
            exps(0, 1, first=True)

            def pair(p, i):
                for b in range(2):
                    g = 2 * (p * PAIRS + i) + b
                    static = isinstance(i, int)
                    ended = static and p == PASSES - 1
                    if not (ended and g + 1 >= ALL):
                        exps(g + 1, 0)
                    if not (ended and g + 2 >= ALL):
                        evac_cT(g + 2, b)
                    if static and i == PAIRS - 1 and b == 1:
                        act.wait_ge(s_pv, CH * g + 1)
                        for k in range(KD):
                            act.copy(sums[:, k, p * HP * P:p * HP * P + CW], acc[k][0][:, :]).then_inc(s_save[0], 1)
                    if not (ended and g + 1 >= ALL):
                        exps(g + 1, 1)

            passes(act, pair, 1)

            for n in range(4):
                kd, half = n // 2, n % 2
                act.wait_ge(s_wvp, n + 1)
                act.copy(wvE[:, kd, 8 * half:8 * half + 8, 0:DH],
                         bank[4 + n][:, :].rearrange("p (h d) -> p h d", h=8)).then_inc(s_wvE, 1)
            act.wait_ge(s_abTp, 1)
            for n in range(2):
                act.mul(abT[:, 2 * n:2 * n + 2, :], bank[4 + n][0:R, :].rearrange("p (n d) -> p n d", n=2),
                        LORA_SCALE).then_inc(s_abT, 1)
            for n in range(4):
                act.wait_ge(s_awp, n + 1)
                act.copy(awE[n][:, :, :], bank[4 + n][:, :].rearrange("p (k d) -> p k d", k=KD)).then_inc(s_awE, 1)
            act.wait_ge(s_attTp, 1)
            act.copy(attT[:, 0:4, :], bank[4][:, :].rearrange("p (m q) -> p m q", m=4)).then_inc(s_attT0, 1)
            act.wait_ge(s_hTp, 1)
            act.copy(hT[:, :, :], bank[1][:, 0:D].rearrange("p (k q) -> p k q", k=KD)).then_inc(s_hT, 1)
            act.wait_ge(s_late, LATE)
            act.wait_ge(s_aqkp, 1)
            for m in range(KD):
                ins = act.activation(aqT[:, m, :], bank[2][:, m * P:(m + 1) * P], ACT.Identity,
                                     bias=abq_col[:, m:m + 1], scale=1.0)
            ins.then_inc(s_aqT, 1)
            act.wait_ge(s_avp, 1)
            act.wait_ge(s_const, 6)
            act.copy(av[:, :, 0:AD], bank[1][:, 0:D].rearrange("p (h d) -> p h d", h=AH)).then_inc(s_av, 1)
            for n in range(4):
                act.wait_ge(s_ashift, n + 1)
                act.activation(a_p[:, 4 * n:4 * n + 4, :], a_p[:, 4 * n:4 * n + 4, :], ACT.Exp,
                               scale=AD ** -0.5).then_inc(s_aexp, 1)
            for n in range(0, 4, 2):
                act.wait_ge(s_apTp, n + 1)
                act.copy(a_pT[:, 4 * n:4 * n + 4, :], bank[n][:, :].rearrange("p (h t) -> p h t", h=4))\
                   .then_inc(s_apT_even, 1)
            act.wait_ge(s_fwTp, 1)
            act.copy(f_wT[:, :, :], bank[7][:, 0:D].bitcast(BF16).rearrange("p (k d) -> p k d", k=KD)).then_inc(s_fwT, 1)
            act.wait_ge(s_aoTp, 1)
            act.copy(aoT[:, :, :], bank[5][:, 0:D].rearrange("p (k q) -> p k q", k=KD)).then_inc(s_aoT, 1)
            act.wait_ge(s_fqTp, 1)
            act.copy(f_qT[:, :, :], bank[0][:, 0:P].bitcast(BF16).rearrange("p (k q) -> p k q", k=KD)).then_inc(s_fqT, 1)
            act.wait_ge(s_y, 1)
            act.dma_start(out_rows, y[:, :]).then_inc(s_out, 16)

        @block.vector
        def _(dve):
            count = [0]

            def link(ins):
                count[0] += 1
                ins.then_inc(s_dstep, 1)
                dve.wait_ge(s_dstep, count[0])

            nvar = [0]

            def normalise(dst, src):
                nvar[0] += 1
                link(dve.bn_stats(stats[:, :], src[:, :]))
                link(dve.bn_aggr(mv[:, :], stats[:, :]))
                dve.tensor_scalar(veps[:, :], mv[:, 1:2], EPS, None, ALU.add).then_inc(s_var, 1)
                dve.wait_ge(s_rstd, nvar[0])
                return dve.tensor_scalar(dst[:, :], src[:, :], mv[:, 0:1], rstd[:, 0:1], ALU.subtract, ALU.mult)

            dve.wait_ge(s_x, 16)
            link(normalise(xn, x_sb))
            normalise(lat, xn).then_inc(s_latn, 1)

            def tile_stats(tiles_of_b, b):
                dve.wait_ge(s_tile[b], 16 * tiles_of_b)
                dve.bn_stats(c_stats[b][:, :], x_tile[b][:, :]).then_inc(s_cst, 1)

            def tile_aggr(g, b, waited=False):
                if not waited:
                    dve.wait_ge(s_cst, g + 1)
                dve.bn_aggr(c_mv[b][:, :], c_stats[b][:, :]).then_inc(s_cag, 1)

            def tile_veps(g, b):
                dve.wait_ge(s_cag, g + 1)
                dve.tensor_scalar(c_veps[b][:, :], c_mv[b][:, 1:2], EPS, None, ALU.add).then_inc(s_cvar, 1)

            def tile_z(g, b, first=False):
                dve.wait_ge(s_crstd, g + 1)
                if not first:
                    dve.wait_ge(s_tr, g - 1)
                    dve.wait_ge(s_zsplit, g - 1)
                dve.tensor_scalar(z[b][:, :], x_tile[b][:, :], c_mv[b][:, 0:1], c_rstd[b][:, 0:1], ALU.subtract,
                                  ALU.mult).then_inc(s_z, 1)

            def split_cT_hi(g, b, first=False):
                dve.wait_ge(s_cT, g + 1)
                if not first:
                    dve.wait_ge(s_scores, CH * (g - 1))
                dve.tensor_copy(cT_hi[b][:, :, :], cT[b][:, :, :]).then_inc(s_cth, 1)

            def split_cT_lo(g, b):
                dve.wait_ge(s_cth, g + 1)
                dve.tensor_tensor(cT_lo[b][:, :, :], cT[b][:, :, :], cT_hi[b][:, :, :].bitcast(F32), ALU.subtract)\
                   .then_inc(s_cTsplit, 1)

            def clip_hi(g, b, c, first=False, stats_of=None):
                dve.wait_ge(s_exp, CH * g + c + 1)
                if not first:
                    dve.wait_ge(s_pv, CH * (g - 2) + c + 1)
                dve.tensor_scalar(p_hi[b][c][:, :], ex[c][:, :], EXP_LO, EXP_HI, ALU.max, ALU.min).then_inc(s_phi, 1)
                if stats_of is not None:
                    dve.wait_ge(s_cst, stats_of + 1)
                dve.tensor_scalar(ex[c][:, :], ex[c][:, :], EXP_LO, EXP_HI, ALU.max, ALU.min).then_inc(s_clip, 1)

            def split_p_lo(g, b, c):
                dve.wait_ge(s_phi, CH * g + c + 1)
                dve.wait_ge(s_clip, CH * g + c + 1)
                dve.tensor_tensor(p_lo[b][c][:, :], ex[c][:, :], p_hi[b][c][:, :].bitcast(F32), ALU.subtract)\
                   .then_inc(s_psplit, 1)

            dve.wait_ge(s_const, 2)
            for g in range(2):
                tile_stats(1, g)
                tile_aggr(g, g)
                tile_veps(g, g)
            for g in range(2):
                tile_z(g, g, first=True)

            dve.wait_ge(s_const, 7)
            dve.wait_ge(s_cols, COLS)
            dve.tensor_copy(identb[:, :], ident[:, :])
            link(dve.scalar_tensor_tensor(neg_w_last[:, :], ctx_w[:, 1:2], -1.0, last_row[:, :], ALU.mult, ALU.mult))
            dve.tensor_scalar(foldT[:, 0, 0:P], ident[:, :], ctx_w[:, 0:1], None, ALU.mult)
            dve.tensor_scalar(foldT[:, 1, 0:P], ident[:, :], 0.0, neg_w_last[:, 0:1], ALU.mult, ALU.add)
            link(dve.tensor_scalar(foldT[:, 1, P:D], ident[:, :], ctx_w[:, 1:2], neg_w_last[:, 0:1], ALU.mult, ALU.add))
            for k in range(KD):
                ins = dve.tensor_copy(foldT[:, k, D - 1:D], ctx_b[:, k:k + 1])
            ins.then_inc(s_foldT, 1)
            dve.memset(wvE[:, 0, :, DH:VW], 0.0)
            dve.tensor_copy(wvE[:, 1, :, DH:VW], last_row[:, 0:1].unsqueeze(1).to_broadcast([P, H, 1])).then_inc(s_wvE, 1)

            for g in range(2):
                split_cT_hi(g, g, first=True)
                split_cT_lo(g, g)
            tile_stats(2, 0)
            tile_aggr(2, 0)
            tile_veps(2, 0)
            tile_z(2, 0)
            dve.wait_ge(s_const, 3)
            for n in range(2):
                dve.wait_ge(s_qTp, n + 1)
                dve.wait_ge(s_qTtop, n + 1)
                dve.tensor_copy(qTbd[DH:P, 4 * n:4 * n + 4, 1, :],
                                bank[4 + n][DH:P, :].rearrange("p (m q) -> p m q", m=4)).then_inc(s_qTbot, 1)
            for n in range(1, 4, 2):
                dve.wait_ge(s_wkTp, n + 1)
                dve.wait_ge(s_wkT, n)
                dve.tensor_copy(wkT[:, 2 * n:2 * n + 2, :], bank[n][:, :].rearrange("p (m d) -> p m d", m=2))\
                   .then_inc(s_wkT, 1)
            order = [4, 5, 0, 1, 2, 3, 4, 5]
            for n in range(8):
                mm, k = n // KD, n % KD
                cols = slice(mm * 512, (mm + 1) * 512)
                dve.wait_ge(s_qkp, n + 1)
                dve.wait_ge(s_qkhi, n + 1)
                dve.tensor_tensor(qk_lo[:, k, cols], bank[order[n]][:, :], qk_hi[:, k, cols].bitcast(F32), ALU.subtract)\
                   .then_inc(s_qklo, 1)
            for c in range(CH):
                clip_hi(0, 0, c, first=True)
                split_p_lo(0, 0, c)

            def pair(p, i):
                for b in range(2):
                    gp = p * PAIRS + i
                    g = 2 * gp + b
                    static = isinstance(i, int)
                    ended = static and p == PASSES - 1
                    more1 = not (ended and g + 1 >= ALL)
                    more2 = not (ended and g + 2 >= ALL)
                    more3 = not (ended and g + 3 >= ALL)
                    start = static and g == 0
                    if more3:
                        tile_stats(gp + 2 + b, 1 - b)
                    if static and i == 0 and b == 0 and p > 0:
                        save_chunk1(p - 1)
                    if more1:
                        clip_hi(g + 1, 1 - b, 0, first=start, stats_of=g + 3 if more3 else None)
                    if more3:
                        tile_aggr(g + 3, 1 - b, waited=True)
                    if more1:
                        split_p_lo(g + 1, 1 - b, 0)
                    if more3:
                        tile_veps(g + 3, 1 - b)
                    if more2:
                        split_cT_hi(g + 2, b)
                    if more3:
                        tile_z(g + 3, 1 - b)
                    if more2:
                        split_cT_lo(g + 2, b)
                    if more1:
                        clip_hi(g + 1, 1 - b, 1, first=start)
                        split_p_lo(g + 1, 1 - b, 1)

            def save_chunk1(p):
                dve.wait_ge(s_pv, CH * TILES * (p + 1))
                for k in range(KD):
                    dve.tensor_copy(sums[:, k, p * HP * P + CW:(p + 1) * HP * P], acc[k][1][:, :])\
                       .then_inc(s_save[1], 1)

            passes(dve, pair, 2)

            save_chunk1(PASSES - 1)

            def per_head(t, n, w):
                return t.unsqueeze(2).to_broadcast([P, n, w])

            dve.wait_ge(s_heads, 1)
            banks_of = [range(j, min(j + HB, H)) for j in range(0, H, HB)]
            for j, hs in enumerate(banks_of):
                o = bank[j][:, 0:len(hs) * VW].rearrange("p (h v) -> p h v", v=VW)
                dve.reciprocal(recip[:, hs[0]:hs[-1] + 1].unsqueeze(2), o[:, :, DH:VW]).then_inc(s_recip, 1)
            for j, hs in enumerate(banks_of):
                o = bank[j][:, 0:len(hs) * VW].rearrange("p (h v) -> p h v", v=VW)
                dve.wait_ge(s_recip, j + 1)
                dve.tensor_tensor(att[:, hs[0]:hs[-1] + 1, :], o[:, :, 0:DH],
                                  per_head(recip[:, hs[0]:hs[-1] + 1], len(hs), DH), ALU.mult).then_inc(s_att, 1)
            dve.wait_ge(s_attTp, 2)
            dve.tensor_copy(attT[:, 4:8, :], bank[5][:, :].rearrange("p (m q) -> p m q", m=4)).then_inc(s_attT1, 1)
            dve.wait_ge(s_xattn, 1)
            link(dve.tensor_tensor(x1[:, :], x_sb[:, :], bank[0][:, 0:D], ALU.add))
            normalise(hn, x1).then_inc(s_hn, 1)
            dve.wait_ge(s_late, LATE)
            dve.wait_ge(s_aqkp, 2)
            for m in range(KD):
                dve.scalar_tensor_tensor(akT[:, m, :, :],
                                         bank[3][:, m * P:(m + 1) * P].unsqueeze(1).to_broadcast([P, HT, P]),
                                         abk_col[:, m:m + 1], per_head(head_mask[:, :], HT, P),
                                         ALU.add, ALU.mult).then_inc(s_akT, 1)
            for n in range(4):
                s_view = bank[4 + n][:, :].rearrange("p (h t) -> p h t", h=4)
                dve.wait_ge(s_ascore, n + 1)
                dve.tensor_reduce(a_max[:, 4 * n:4 * n + 4], s_view, AX_X, ALU.max).then_inc(s_amax, 1)
                dve.wait_ge(s_amax, n + 1)
                dve.tensor_tensor(a_p[:, 4 * n:4 * n + 4, :], s_view, per_head(a_max[:, 4 * n:4 * n + 4], 4, P),
                                  ALU.subtract).then_inc(s_ashift, 1)
            link(dve.tensor_copy(f_u[:, :, :], f_bytes[:, :, :]))
            dve.tensor_scalar(f_mag[:, :, :], f_u[:, :, :], 0x7F, 7, ALU.bitwise_and, ALU.logical_shift_left)
            link(dve.tensor_scalar(f_sgn[:, :, :], f_u[:, :, :], 0x80, 8, ALU.bitwise_and, ALU.logical_shift_left))
            link(dve.tensor_tensor(f_h[:, :, :], f_mag[:, :, :], f_sgn[:, :, :], ALU.bitwise_or))
            dve.tensor_scalar(f_w[:, :, :], f_h[:, :, :].bitcast(FP16), 256.0, None, ALU.mult).then_inc(s_fw, 1)
            for n in range(1, 4, 2):
                dve.wait_ge(s_apTp, n + 1)
                dve.tensor_copy(a_pT[:, 4 * n:4 * n + 4, :], bank[n][:, :].rearrange("p (h t) -> p h t", h=4))\
                   .then_inc(s_apT_odd, 1)
            dve.wait_ge(s_apv, 1)
            o = bank[4][:, 0:AH * (AD + 1)].rearrange("p (h v) -> p h v", v=AD + 1)
            link(dve.reciprocal(a_recip[:, :].unsqueeze(2), o[:, :, AD:AD + 1]))
            dve.tensor_tensor(ao[:, :, :], o[:, :, 0:AD], per_head(a_recip[:, :], AH, AD), ALU.mult).then_inc(s_ao, 1)
            dve.wait_ge(s_attn, 1)
            link(dve.tensor_tensor(x2[:, :], x1[:, :], bank[6][:, 0:D], ALU.add))
            link(normalise(fn, x2))
            link(dve.tensor_reduce(amax[:, :], fn[:, :], AX_X, ALU.max, apply_absolute_value=True))
            link(dve.tensor_scalar(f_xs[:, :], amax[:, :], 1e-12, 1.0 / FP8_MAX, ALU.max, ALU.mult))
            link(dve.reciprocal(f_inv[:, :], f_xs[:, :]))
            link(dve.tensor_scalar(fv[:, :], fn[:, :], f_inv[:, 0:1], None, ALU.mult))
            link(dve.tensor_scalar(f_pow[:, :].bitcast(I32), fv[:, :].bitcast(I32), 0x7F800000, None, ALU.bitwise_and))
            link(dve.tensor_scalar(f_magic[:, :], f_pow[:, :], 2.0 ** -6, 1.5 * 2.0 ** 20, ALU.max, ALU.mult))
            link(dve.tensor_tensor(f_sum[:, :], fv[:, :], f_magic[:, :], ALU.add))
            dve.tensor_tensor(f_q[:, :], f_sum[:, :], f_magic[:, :], ALU.subtract).then_inc(s_fq, 1)
            dve.tensor_tensor(f_row_scale[:, :], f_xs[:, :], f_ws[:, :], ALU.mult)
            link(dve.tensor_tensor(x2b[:, :], x2[:, :], f_b[:, :], ALU.add))
            dve.wait_ge(s_ffn, 1)
            dve.scalar_tensor_tensor(y[:, :], bank[1][:, 0:D], f_row_scale[:, 0:1], x2b[:, :], ALU.mult, ALU.add)\
               .then_inc(s_y, 1)


_INS = ['x', 'ctx_1024', 'L0_xattn_ln_l_w', 'L0_xattn_ln_l_b', 'L0_xattn_ln_c_w', 'L0_xattn_ln_c_b', 'L0_xattn_Wq',
        'L0_xattn_Wkv', 'L0_xattn_Wo', 'L0_xattn_bo',
        'L0_attn_Wq', 'L0_attn_bq', 'L0_attn_Aq', 'L0_attn_Bq', 'L0_attn_Wk', 'L0_attn_bk', 'L0_attn_Ak', 'L0_attn_Bk',
        'L0_attn_Wv', 'L0_attn_bv', 'L0_attn_Av', 'L0_attn_Bv', 'L0_attn_Wo', 'L0_attn_bo', 'L0_attn_Ao', 'L0_attn_Bo',
        'L0_ffn_weight', 'L0_ffn_weight_scale', 'L0_ffn_bias']
_OUTS = [((1, 128, 256), 'float32')]


def kernel(**inputs):
    import concourse.bacc as _bacc
    from concourse.bass_utils import run_bass_kernel_spmd as _run

    nc = _bacc.Bacc("TRN2", target_bir_lowering=False, num_devices=1)
    arrays, args = {}, []
    for name in _INS:
        a = np.ascontiguousarray(inputs[name])
        arrays[f"in_{name}_dram"] = a
        args.append(nc.dram_tensor(f"in_{name}_dram", a.shape, mybir.dt.from_np(a.dtype), kind="ExternalInput").ap())
    for i, (shape, dtype) in enumerate(_OUTS):
        dt = mybir.dt.from_np(np.dtype(dtype))
        args.append(nc.dram_tensor(f"out_{i}_dram", shape, dt, kind="ExternalOutput").ap())
    perceiver_layer(nc, *args)
    r = _run(nc, [arrays], core_ids=[0])
    return r.results[0]["out_0_dram"]
```

```python
from contextlib import ExitStack

import numpy as np
import concourse.bass as bass
from concourse import mybir

ALU = mybir.AluOpType
ACT = mybir.ActivationFunctionType
AX_X = mybir.AxisListType.X
F32 = mybir.dt.float32
F32R = mybir.dt.float32r
BF16 = mybir.dt.bfloat16
U8 = mybir.dt.uint8
U16 = mybir.dt.uint16
I32 = mybir.dt.int32
FP16 = mybir.dt.float16

P = 128
EPS = 1e-5
FP8_MAX = 448.0
LORA_SCALE = 2.0


def perceiver_layer(
    nc, x, ctx, ln_l_w, ln_l_b, ln_c_w, ln_c_b, Wq, Wkv, Wo, bo,
    aWq, abq, aAq, aBq, aWk, abk, aAk, aBk, aWv, abv, aAv, aBv, aWo, abo, aAo, aBo,
    f_weight, f_scale, f_bias, out,
):
    _, N, D = x.shape
    S = ctx.shape[1]
    INNER = Wq.shape[1]
    H = 16
    DH = INNER // H
    KD = D // P
    MI = INNER // P
    TILES = S // P
    PAIRS = TILES // 2
    PASSES = 2
    HP = H // PASSES
    CH = 2
    CW = HP * P // CH
    HC = HP // CH
    ALL = PASSES * TILES
    SCALE = DH ** -0.5
    EXP_LO, EXP_HI = (float(np.float32(np.exp(np.float64(s)))) for s in (-11.0, 11.0))
    AH = 16
    AD = D // AH
    R = aAq.shape[0]
    HT = P // AD
    VW = DH + 1
    HB = 512 // VW
    assert N == P and S == TILES * P and TILES == 2 * PAIRS and D == 2 * P

    with ExitStack() as stack:
        def sb(name, shape, dt=F32):
            return stack.enter_context(nc.sbuf_tensor(name, shape, dt))

        def sem(name):
            return stack.enter_context(nc.semaphore(name))

        bank = [stack.enter_context(nc.psum_tensor(f"bank{n}", [P, 512], F32)) for n in range(8)]
        acc = [[bank[k * CH + c] for c in range(CH)] for k in range(KD)]
        sc_bank = bank[4:6]
        tr_bank = bank[6:8]

        ident = sb("ident", [P, P])
        identb = sb("identb", [P, P], BF16)
        ones = sb("ones", [P, D])
        ones_row = ones[0:1, 0:P]
        last_row = sb("last_row", [P, 1])
        neg_half = sb("neg_half", [P, 1])
        warm = sb("warm", [P, 1])
        head_mask = sb("head_mask", [P, HT])

        x_sb = sb("x_sb", [P, D])
        lat_w, lat_b = sb("lat_w", [P, KD]), sb("lat_b", [P, KD])
        ctx_w, ctx_b = sb("ctx_w", [P, KD]), sb("ctx_b", [P, KD])
        xn = sb("xn", [P, D])
        lat = sb("lat", [P, D])
        stats = sb("stats", [P, 6])
        mv = sb("mv", [P, 2])
        veps = sb("veps", [P, 1])
        rstd = sb("rstd", [P, 1])
        latT = sb("latT", [P, KD, P])
        qk_hi = sb("qk_hi", [P, KD, H * P], F32R)
        qk_lo = sb("qk_lo", [P, KD, H * P], F32R)

        x_tile = [sb(f"x_tile{b}", [P, D]) for b in range(2)]
        c_stats = [sb(f"c_stats{b}", [P, 6]) for b in range(2)]
        c_mv = [sb(f"c_mv{b}", [P, 2]) for b in range(2)]
        c_veps = [sb(f"c_veps{b}", [P, 1]) for b in range(2)]
        c_rstd = [sb(f"c_rstd{b}", [P, 1]) for b in range(2)]
        z = [sb(f"z{b}", [P, D]) for b in range(2)]
        z_hi = [sb(f"z_hi{b}", [P, D], F32R) for b in range(2)]
        z_lo = [sb(f"z_lo{b}", [P, D], F32R) for b in range(2)]
        cT_all = sb("cT_all", [P, TILES, KD, P])
        cT_hi = [sb(f"cT_hi{b}", [P, KD, P], F32R) for b in range(2)]
        cT_lo = [sb(f"cT_lo{b}", [P, KD, P], F32R) for b in range(2)]
        ex = [sb(f"ex{c}", [P, CW]) for c in range(CH)]
        p_hi = [[sb(f"p_hi{b}{c}", [P, CW], F32R) for c in range(CH)] for b in range(2)]
        p_lo = [[sb(f"p_lo{b}{c}", [P, CW], F32R) for c in range(CH)] for b in range(2)]
        sums = sb("sums", [P, KD, H * P])
        foldT = sb("foldT", [P, KD, D])
        neg_w_last = sb("neg_w_last", [P, 1])
        av = sb("av", [P, AH, AD + 1])
        recip = sb("recip", [P, H])
        a_k1 = sb("a_k1", [P, P])
        a_max = sb("a_max", [P, AH])
        a_recip = sb("a_recip", [P, AH])
        amax = sb("amax", [P, 1])
        f_xs = sb("f_xs", [P, 1])
        f_inv = sb("f_inv", [P, 1])
        f_row_scale = sb("f_row_scale", [P, 1])
        f_ws = sb("f_ws", [P, 1])
        f_q = sb("f_q", [P, D], BF16)
        f_qT = sb("f_qT", [P, KD, P], BF16)
        f_bytes = sb("f_bytes", [P, KD, D], U8)
        f_w = sb("f_w", [P, KD, D], BF16)
        f_wT = sb("f_wT", [P, KD, D], BF16)
        abq_col, abk_col = sb("abq_col", [P, KD]), sb("abk_col", [P, KD])

        flat = cT_all[:, :, :, :].rearrange("p t k q -> p (t k q)")
        end = [TILES * D]
        used = [0]

        def from_end(n):
            end[0] -= n
            return flat[:, end[0]:end[0] + n]

        def from_start(n, rows=P):
            used[0] += n
            return flat[0:rows, used[0] - n:used[0]]

        wq = from_end(KD * INNER).rearrange("p (k n) -> p k n", k=KD)
        wk = from_end(KD * INNER).rearrange("p (k n) -> p k n", k=KD)
        qTbd = from_end(MI * 2 * P).rearrange("p (m a q) -> p m a q", m=MI, a=2)
        wkT = from_end(MI * D).rearrange("p (m d) -> p m d", m=MI)
        PROLOGUE_TILE = end[0] // D
        att = wk[:, 0, :].rearrange("p (h d) -> p h d", h=H)
        attT = wk[:, 1, :].rearrange("p (m q) -> p m q", m=MI)
        akT = wkT.rearrange("p m d -> p (m d)").rearrange("p (k h t) -> p k h t", k=KD, h=HT)
        a_p = wq.rearrange("p k n -> p (k n)").rearrange("p (h t) -> p h t", h=AH)
        a_pT = qTbd.rearrange("p m a q -> p (m a) q")

        wv = from_start(KD * INNER).rearrange("p (k n) -> p k n", k=KD)
        wo = from_start(MI * D).rearrange("p (m n) -> p m n", m=MI)
        bo_row = from_start(D, 1)
        aw = [from_start(KD * D).rearrange("p (k n) -> p k n", k=KD) for n in range(4)]
        aa_all = from_start(4 * D, R)
        aa = [aa_all[:, n * D:(n + 1) * D] for n in range(4)]
        abT = [from_start(D, R) for n in range(4)]
        abv_row, abo_row = from_start(D, 1), from_start(D, 1)
        f_b = from_start(D)
        LATE_TILE = -(-used[0] // D)
        wvE = from_start(KD * H * VW).rearrange("p (k h v) -> p k h v", k=KD, h=H)
        awE = [from_start(KD * D).rearrange("p (k n) -> p k n", k=KD) for n in range(4)]
        x1, hn, x2, x2b, fn, fv, f_pow, f_magic, f_sum, y = (
            sb(n, [P, D]) for n in ("x1", "hn", "x2", "x2b", "fn", "fv", "f_pow", "f_magic", "f_sum", "y"))
        hT, aqT, aoT = (sb(n, [P, KD, P]) for n in ("hT", "aqT", "aoT"))
        ao = sb("ao", [P, AH, AD])
        f_u = sb("f_u", [P, KD, D], U16)
        f_mag, f_sgn = (t[:, :].bitcast(U16).rearrange("p (k d) -> p k d", k=KD) for t in (xn, lat))
        f_h = latT[:, :, :].rearrange("p k q -> p (k q)").bitcast(U16).rearrange("p (k d) -> p k d", k=KD)
        assert used[0] <= end[0] and LATE_TILE < TILES - 20

        s_x = sem("x_loaded")
        s_cols = sem("cols_loaded")
        s_wq = sem("wq_loaded")
        s_wk = sem("wk_loaded")
        s_late = sem("late_weights_loaded")
        s_const = sem("pool_constants_ready")
        s_dstep = sem("dve_step_done")
        s_pstep = sem("pool_step_done")
        s_var = sem("variance_ready")
        s_rstd = sem("rstd_ready")
        s_latn = sem("lat_normalised")
        s_latTp = sem("lat_transposed")
        s_latT = sem("latT_ready")
        s_wkTp = sem("wk_transposed")
        s_wkT = sem("wkT_ready")
        s_qTp = sem("qT_computed")
        s_qTtop = sem("qT_upper_heads_ready")
        s_qTbot = sem("qT_lower_heads_ready")
        s_qkp = sem("qk_computed")
        s_qkhi = sem("qk_hi_ready")
        s_qklo = sem("qk_lo_ready")
        s_tile = [sem(f"ctx_tile{b}_loaded") for b in range(2)]
        s_cvar = sem("ctx_variance_ready")
        s_crstd = sem("ctx_rstd_ready")
        s_z = sem("z_ready")
        s_zsplit = sem("z_split_ready")
        s_tr = sem("z_transposed")
        s_cT = sem("cT_stored")
        s_cTsplit = sem("cT_split_ready")
        s_scores = sem("scores_ready")
        s_exp = sem("exp_ready")
        s_psplit = sem("probs_split_ready")
        s_pv = sem("pv_done")
        s_save = [sem(f"sums_saved{c}") for c in range(CH)]
        s_foldT = sem("foldT_ready")
        s_wvp = sem("wvE_computed")
        s_wvE = sem("wvE_ready")
        s_wvden = sem("wvE_denominator_column_ready")
        s_zhi = sem("z_hi_ready")
        s_cst = sem("ctx_stats_ready")
        s_cag = sem("ctx_mean_var_ready")
        s_cth = sem("cT_hi_ready")
        s_phi = sem("probs_hi_ready")
        s_clip = sem("probs_clipped")
        s_heads = sem("head_outputs_computed")
        s_lora = sem("loraA_scaled")
        s_awp = [sem(f"attn_weights_{n}_computed") for n in "qkvo"]
        s_awE = [sem(f"attn_weights_{n}_ready") for n in "qkvo"]
        s_recip = sem("denominators_inverted")
        s_att = sem("head_outputs_normalised")
        s_attTp = sem("head_outputs_transposed")
        s_attT0 = sem("attT_heads_0_7_ready")
        s_attT1 = sem("attT_heads_8_15_ready")
        s_xattn = sem("cross_attention_computed")
        s_hn = sem("h_normalised")
        s_hTp = sem("h_transposed")
        s_hT = sem("hT_ready")
        s_akp = sem("self_k_computed")
        s_aqp = sem("self_q_computed")
        s_ak1 = sem("self_kT_heads_8_15_with_bias")
        s_avp = sem("self_v_computed")
        s_aqT = sem("self_qT_ready")
        s_akT = [sem(f"self_kT_half{m}_ready") for m in range(KD)]
        s_av = sem("self_v_ready")
        s_ascore = sem("self_scores_computed")
        s_amax = sem("self_max_ready")
        s_ashift = sem("self_scores_shifted")
        s_aexp = sem("self_exp_ready")
        s_apTp = sem("self_probs_transposed")
        s_apT = sem("self_probsT_banks_0_1_3_ready")
        s_apT2 = sem("self_probsT_bank_2_ready")
        s_apv = sem("self_outputs_computed")
        s_ao = sem("self_outputs_normalised")
        s_aoTp = sem("self_outputs_transposed")
        s_aoT = sem("self_outputsT_ready")
        s_attn = sem("self_attention_computed")
        s_fw = sem("fp8_weights_decoded")
        s_fwTp = sem("fp8_weights_transposed")
        s_fwT = sem("fp8_weightsT_ready")
        s_fq = sem("fp8_rows_rounded")
        s_fqTp = sem("fp8_rows_transposed")
        s_fqT = sem("fp8_rowsT_ready")
        s_ffn = sem("fp8_linear_computed")
        s_y = sem("y_ready")
        s_out = sem("out_stored")

        LATE = 16 * (3 + 4 * 3 + 4 + 3)
        COLS = 16 * 4

        def col(v):
            return v.rearrange("(k p) -> p k", p=P)

        def row(v):
            return v.rearrange("(a d) -> a d", a=1)

        def rows(w):
            return w.rearrange("(k p) n -> p k n", p=P)

        x_rows = x.rearrange("a n d -> (a n) d")
        out_rows = out.rearrange("a n d -> (a n) d")
        ctx_rows = ctx.rearrange("a s d -> (a s) d")
        wkv = rows(Wkv)

        block = stack.enter_context(nc.Block())

        AW_BANK = (4, 5, 3, 3)
        UNROLL = 4
        LOOPED = (PAIRS - 1 - 2) // UNROLL * UNROLL

        def passes(eng, pair):
            for p in range(PASSES):
                pair(p, 0)
                with eng.Fori(1, 1 + LOOPED, UNROLL) as i:
                    for u in range(UNROLL):
                        pair(p, i + u)
                for i in range(1 + LOOPED, PAIRS):
                    pair(p, i)

        @block.sync
        def _(sp):
            sp.dma_start(x_sb[:, :], x_rows).then_inc(s_x, 16)
            sp.dma_start(wk[:, :, :], wkv[:, :, 0:INNER]).then_inc(s_wk, 16)
            for b in range(2):
                sp.dma_start(x_tile[b][:, :], ctx_rows[b * P:(b + 1) * P, :]).then_inc(s_tile[b], 16)
            sp.dma_start(wq[:, :, :], rows(Wq)).then_inc(s_wq, 16)

            def load(p, i):
                for b in range(2):
                    sp.wait_ge(s_z, 2 * (p * PAIRS + i) + b - 1)
                    sp.dma_start(x_tile[b][:, :], ctx_rows[bass.ds((2 * i + b) * P, P), :]).then_inc(s_tile[b], 16)

            def late(dst, src):
                sp.dma_start(dst, src, allow_slow_non_contiguous=True).then_inc(s_late, 16)

            scale_all = bass.AP(f_scale.tensor, 0, [[0, P], [1, 1]])
            bias_all = bass.AP(f_bias.tensor, 0, [[0, P], [1, D]])
            late_loads = [(wv, wkv[:, :, INNER:2 * INNER]), (wo, rows(Wo)), (bo_row, row(bo))]
            for n, (w, a, b_) in enumerate(((aWq, aAq, aBq), (aWk, aAk, aBk), (aWv, aAv, aBv), (aWo, aAo, aBo))):
                late_loads += [(aw[n], rows(w)), (aa[n], a), (abT[n], b_.rearrange("d r -> r d"))]
            late_loads += [(abq_col[:, :], col(abq)), (abk_col[:, :], col(abk)), (abv_row, row(abv)),
                           (abo_row, row(abo)), (f_bytes[:, :, :], rows(f_weight.bitcast(U8))),
                           (f_ws[:, :], scale_all), (f_b, bias_all)]
            assert 16 * len(late_loads) == LATE

            with sp.Fori(1, PAIRS) as i:
                load(0, i)
            FREE = LATE_TILE // 2 + 1
            load(1, 0)
            with sp.Fori(1, FREE + 1) as i:
                load(1, i)
            sp.wait_ge(s_cTsplit, TILES + LATE_TILE)
            at = 0
            for i in range(FREE + 1, FREE + 1 + 7):
                load(1, i)
                for dst, src in late_loads[at:at + 4]:
                    late(dst, src)
                at += 4
            assert at >= len(late_loads)
            with sp.Fori(FREE + 8, PAIRS) as i:
                load(1, i)

            sp.wait_ge(s_out, 16)

        @block.gpsimd
        def _(pool):
            steps = [0]

            def const_step(ins):
                steps[0] += 1
                ins.then_inc(s_pstep, 1)
                pool.wait_ge(s_pstep, steps[0])

            const_step(pool.memset(ident[:, :], 0.0))
            pool.affine_select(out=ident[:, :], in_=ident[:, :], compare_op=ALU.not_equal, fill=1.0, base=0,
                               pattern=[[-1, P]], channel_multiplier=1).then_inc(s_const, 1)
            pool.memset(neg_half[:, :], -0.5).then_inc(s_const, 1)
            pool.memset(qTbd[:, :, :, :], 0.0).then_inc(s_const, 1)

            def inv_sqrt(n):
                pool.wait_ge(s_var, n)
                pool.tensor_tensor(rstd[:, :], veps[:, :], neg_half[:, :], ALU.pow).then_inc(s_rstd, 1)

            def ctx_rstd(g, b):
                pool.wait_ge(s_cvar, g + 1)
                pool.tensor_tensor(c_rstd[b][:, :], c_veps[b][:, :], neg_half[:, :], ALU.pow).then_inc(s_crstd, 1)

            const_step(pool.memset(ones[:, :], 1.0))
            inv_sqrt(1)
            inv_sqrt(2)
            for b in range(2):
                const_step(pool.memset(z_hi[b][:, D - 1:D].bitcast(F32), 1.0))
                const_step(pool.memset(z_lo[b][:, D - 1:D].bitcast(F32), 0.0))
            const_step(pool.memset(last_row[:, :], 0.0))
            pool.affine_select(out=last_row[:, :], in_=last_row[:, :], compare_op=ALU.not_equal, fill=1.0,
                               base=-(P - 1), pattern=[[0, 1]], channel_multiplier=1).then_inc(s_const, 1)
            const_step(pool.memset(head_mask[:, :], 1.0))
            const_step(pool.affine_select(out=head_mask[:, :], in_=head_mask[:, :], compare_op=ALU.is_ge, fill=0.0,
                                          base=0, pattern=[[-AD, HT]], channel_multiplier=1))
            pool.affine_select(out=head_mask[:, :], in_=head_mask[:, :], compare_op=ALU.is_ge, fill=0.0,
                               base=AD - 1, pattern=[[AD, HT]], channel_multiplier=-1).then_inc(s_const, 1)
            pool.memset(av[:, :, AD:AD + 1], 1.0).then_inc(s_const, 1)
            pool.memset(foldT[:, 0, P:D], 0.0).then_inc(s_const, 1)

            def split_z(g, b, first=False):
                pool.wait_ge(s_z, g + 1)
                if not first:
                    pool.wait_ge(s_pv, CH * (g - 1))
                pool.tensor_tensor(z_hi[b][:, 0:D - 1], z[b][:, 0:D - 1], ones[:, 0:D - 1], ALU.mult).then_inc(s_zhi, 1)
                pool.wait_ge(s_zhi, g + 1)
                pool.tensor_tensor(z_lo[b][:, 0:D - 1], z[b][:, 0:D - 1], z_hi[b][:, 0:D - 1].bitcast(F32),
                                   ALU.subtract).then_inc(s_zsplit, 1)

            for g in range(2):
                ctx_rstd(g, g)
            split_z(0, 0, first=True)
            ctx_rstd(2, 0)

            def pair(p, i):
                for b in range(2):
                    g = 2 * (p * PAIRS + i) + b
                    last = p == PASSES - 1 and isinstance(i, int)
                    if not (last and g + 1 >= ALL):
                        split_z(g + 1, 1 - b, first=(p == 0 and isinstance(i, int) and g == 0))
                    if not (last and g + 3 >= ALL):
                        ctx_rstd(g + 3, 1 - b)

            passes(pool, pair)
            inv_sqrt(3)
            pool.wait_ge(s_ak1, 1)
            pool.wait_ge(s_const, 6)
            pool.tensor_tensor(akT[:, 1, :, :], a_k1[:, :].unsqueeze(1).to_broadcast([P, HT, P]),
                               head_mask[:, :].unsqueeze(2).to_broadcast([P, HT, P]), ALU.mult).then_inc(s_akT[1], 1)
            inv_sqrt(4)

        @block.tensor
        def _(pe):
            def mm3(dst, hi, lo, mhi, mlo, start, stop):
                pe.matmul(dst, hi, mhi, start=start, stop=False)
                pe.matmul(dst, hi, mlo, start=False, stop=False)
                return pe.matmul(dst, lo, mhi, start=False, stop=stop)

            def transpose_z(g, b, first=False):
                pe.wait_ge(s_z, g + 1)
                if not first:
                    pe.wait_ge(s_cT, g - 1)
                for k in range(KD):
                    ins = pe.transpose(tr_bank[b][:, k * P:(k + 1) * P], z[b][:, k * P:(k + 1) * P], ident[:, :])
                ins.then_inc(s_tr, 1)

            def scores(p, g, b, c, first=False):
                pe.wait_ge(s_cTsplit, g + 1)
                if not first:
                    pe.wait_ge(s_exp, CH * (g - 1) + c + 1)
                cols = slice(p * HP * P + c * CW, p * HP * P + (c + 1) * CW)
                for k in range(KD):
                    ins = mm3(sc_bank[c][:, :], cT_hi[b][:, k, :], cT_lo[b][:, k, :], qk_hi[:, k, cols],
                              qk_lo[:, k, cols], k == 0, k == KD - 1)
                ins.then_inc(s_scores, 1)

            def weighted_sum(g, b, c, start, stop, saved=0):
                pe.wait_ge(s_psplit, CH * g + c + 1)
                if c == 0:
                    pe.wait_ge(s_zsplit, g + 1)
                if saved:
                    pe.wait_ge(s_save[c], saved)
                for k in range(KD):
                    ks = slice(k * P, (k + 1) * P)
                    ins = mm3(acc[k][c][:, :], z_hi[b][:, ks], z_lo[b][:, ks], p_hi[b][c][:, :], p_lo[b][c][:, :],
                              start, stop)
                ins.then_inc(s_pv, 1)

            pe.wait_ge(s_const, 1)
            pe.wait_ge(s_latn, 1)
            for k in range(KD):
                ins = pe.transpose(bank[4][:, k * P:(k + 1) * P], lat[:, k * P:(k + 1) * P], ident[:, :])
            ins.then_inc(s_latTp, 1)
            pe.wait_ge(s_wk, 16)
            for m in range(MI):
                for k in range(KD):
                    ins = pe.transpose(bank[m // 2][:, (m % 2) * D + k * P:(m % 2) * D + (k + 1) * P],
                                       wk[:, k, m * P:(m + 1) * P], ident[:, :])
                if m % 2 == 1:
                    ins.then_inc(s_wkTp, 1)
            pe.wait_ge(s_wq, 16)
            pe.wait_ge(s_latT, KD)
            for m in range(MI):
                for k in range(KD):
                    ins = pe.matmul(bank[4 + m // 4][:, (m % 4) * P:(m % 4 + 1) * P], wq[:, k, m * P:(m + 1) * P],
                                    latT[:, k, :], start=(k == 0), stop=(k == KD - 1))
                if m % 4 == 3:
                    ins.then_inc(s_qTp, 1)
            transpose_z(0, 0, first=True)
            transpose_z(1, 1, first=True)
            for n in range(MI // 2 * KD):
                mm, k = n // KD, n % KD
                pe.wait_ge(s_wkT, max(mm + 1, n % 4 + 1))
                pe.wait_ge(s_qTtop, mm // 2 + 1)
                pe.wait_ge(s_qTbot, mm // 2 + 1)
                if n >= 4:
                    pe.wait_ge(s_qklo, n - 3)
                for j in range(2):
                    m = 2 * mm + j
                    ins = pe.matmul(bank[n % 4][:, j * 2 * P:(j + 1) * 2 * P], wkT[:, m, k * P:(k + 1) * P],
                                    qTbd[:, m, :, :].rearrange("p a q -> p (a q)"), start=True, stop=True)
                ins.then_inc(s_qkp, 1)

            pe.wait_ge(s_qklo, 4)
            for c in range(CH):
                scores(0, 0, 0, c, first=True)
            pe.wait_ge(s_qklo, 8)

            def pair(p, i):
                for b in range(2):
                    g = 2 * (p * PAIRS + i) + b
                    static = isinstance(i, int)
                    next_p = p + 1 if static and i == PAIRS - 1 and b == 1 else p
                    first = static and i == 0 and b == 0
                    last = static and i == PAIRS - 1 and b == 1
                    ended = static and p == PASSES - 1
                    for c in range(CH):
                        if c == 0 and p == 0 and not (static and i == PAIRS - 1):
                            transpose_z(g + 2, b)
                        if not (ended and g + 1 >= ALL):
                            scores(next_p, g + 1, 1 - b, c)
                        weighted_sum(g, b, c, first, last, saved=p * KD if first else 0)

            passes(pe, pair)

            pe.wait_ge(s_late, LATE)
            pe.wait_ge(s_foldT, 1)
            pe.wait_ge(s_exp, CH * ALL)
            pe.wait_ge(s_cT, TILES)
            for n in range(4):
                half, kd = n // 2, n % 2
                for k in range(KD):
                    ins = pe.matmul(bank[4 + n][:, :], foldT[:, k, kd * P:(kd + 1) * P],
                                    wv[:, k, half * 512:(half + 1) * 512], start=(k == 0), stop=(k == KD - 1))
                ins.then_inc(s_wvp, 1)
            for c in range(CH):
                pe.wait_ge(s_save[c], PASSES * KD)
            for h in range(H):
                if h % (H // 2) == 0:
                    pe.wait_ge(s_wvden, 1)
                    pe.wait_ge(s_wvE, 2 + 2 * (h // (H // 2)))
                o = bank[h // HB][:, (h % HB) * VW:(h % HB + 1) * VW]
                for k in range(KD):
                    ins = pe.matmul(o, sums[:, k, h * P:(h + 1) * P], wvE[:, k, h, :], start=(k == 0),
                                    stop=(k == KD - 1))
                if h % HB == HB - 1 or h == H - 1:
                    ins.then_inc(s_heads, 1)

            def effective_weights(n):
                for k in range(KD):
                    for m in range(KD):
                        dst = bank[AW_BANK[n]][:, k * D + m * P:k * D + (m + 1) * P]
                        pe.matmul(dst, aw[n][:, m, k * P:(k + 1) * P], ident[:, :], start=True, stop=False,
                                  is_transpose=True)
                        ins = pe.matmul(dst, aa[n][:, k * P:(k + 1) * P], abT[n][:, m * P:(m + 1) * P],
                                        start=False, stop=True)
                ins.then_inc(s_awp[n], 1)

            for m in range(MI):
                if m in (0, MI - 1):
                    pe.wait_ge(s_att, 2 if m == 0 else 3)
                ins = pe.transpose(bank[4 + m // 4][:, (m % 4) * P:(m % 4 + 1) * P],
                                   att[:, :, :].rearrange("p h d -> p (h d)")[:, m * P:(m + 1) * P], ident[:, :])
                if m % 4 == 3:
                    ins.then_inc(s_attTp, 1)
            pe.matmul(bank[0][:, 0:D], ones_row[:, :], bo_row[:, :], start=True, stop=False)
            for m in range(MI):
                if m == 0:
                    pe.wait_ge(s_attT0, 1)
                if m == MI // 2:
                    pe.wait_ge(s_attT1, 1)
                ins = pe.matmul(bank[0][:, 0:D], attT[:, m, :], wo[:, m, :], start=False, stop=(m == MI - 1))
            ins.then_inc(s_xattn, 1)
            pe.wait_ge(s_lora, 1)
            effective_weights(1)
            effective_weights(0)
            pe.wait_ge(s_hn, 1)
            for k in range(KD):
                ins = pe.transpose(bank[1][:, k * P:(k + 1) * P], hn[:, k * P:(k + 1) * P], ident[:, :])
            ins.then_inc(s_hTp, 1)
            pe.wait_ge(s_hT, 1)
            for n, banks, done in ((1, (3, 1), s_akp), (0, (2, 2), s_aqp)):
                pe.wait_ge(s_awE[n], 1)
                for m in range(KD):
                    for k in range(KD):
                        ins = pe.matmul(bank[banks[m]][:, m * P:(m + 1) * P], awE[n][:, k, m * P:(m + 1) * P],
                                        hT[:, k, :], start=(k == 0), stop=(k == KD - 1))
                ins.then_inc(done, 1)
            pe.wait_ge(s_aqT, 1)
            for n in range(4):
                m, half = n // 2, n % 2
                if half == 0:
                    pe.wait_ge(s_akT[m], 1)
                pe.matmul(bank[4 + n][:, :], aqT[:, m, :],
                          akT[:, m, 4 * half:4 * half + 4, :].rearrange("p h t -> p (h t)"),
                          start=True, stop=True).then_inc(s_ascore, 1)
            effective_weights(2)

            def transposed_probs(n):
                pe.wait_ge(s_aexp, n + 1)
                for j in range(4):
                    ins = pe.transpose(bank[n][:, j * P:(j + 1) * P], a_p[:, 4 * n + j, :], ident[:, :])
                ins.then_inc(s_apTp, 1)

            transposed_probs(0)
            transposed_probs(1)
            pe.wait_ge(s_awE[2], 1)
            pe.wait_ge(s_ashift, 2)
            for k in range(KD):
                pe.matmul(bank[5][:, 0:D], hT[:, k, :], awE[2][:, k, :], start=(k == 0), stop=False)
            pe.matmul(bank[5][:, 0:D], ones_row[:, :], abv_row[:, :], start=False, stop=True).then_inc(s_avp, 1)
            transposed_probs(2)
            transposed_probs(3)
            pe.wait_ge(s_av, 1)
            for h in range(AH):
                if h % 4 == 0:
                    pe.wait_ge(*((s_apT, 1), (s_apT, 2), (s_apT2, 1), (s_apT, 3))[h // 4])
                ins = pe.matmul(bank[4][:, h * (AD + 1):(h + 1) * (AD + 1)], a_pT[:, h, :], av[:, h, :],
                                start=True, stop=True)
            ins.then_inc(s_apv, 1)
            effective_weights(3)
            pe.wait_ge(s_ao, 1)
            for k in range(KD):
                ins = pe.transpose(bank[5][:, k * P:(k + 1) * P],
                                   ao[:, :, :].rearrange("p h d -> p (h d)")[:, k * P:(k + 1) * P], ident[:, :])
            ins.then_inc(s_aoTp, 1)
            pe.matmul(bank[6][:, 0:D], ones_row[:, :], abo_row[:, :], start=True, stop=False)
            pe.wait_ge(s_aoT, 1)
            pe.wait_ge(s_awE[3], 1)
            for k in range(KD):
                ins = pe.matmul(bank[6][:, 0:D], aoT[:, k, :], awE[3][:, k, :], start=False, stop=(k == KD - 1))
            ins.then_inc(s_attn, 1)
            pe.wait_ge(s_fw, 1)
            fw_bank = bank[7][:, :].bitcast(BF16)
            for m in range(KD):
                for k in range(KD):
                    ins = pe.transpose(fw_bank[:, k * D + m * P:k * D + (m + 1) * P], f_w[:, m, k * P:(k + 1) * P],
                                       identb[:, :])
            ins.then_inc(s_fwTp, 1)
            pe.wait_ge(s_fq, 1)
            fq_bank = bank[0][:, :].bitcast(BF16)
            for k in range(KD):
                ins = pe.transpose(fq_bank[:, k * P:(k + 1) * P], f_q[:, k * P:(k + 1) * P], identb[:, :])
            ins.then_inc(s_fqTp, 1)
            pe.wait_ge(s_fqT, 1)
            pe.wait_ge(s_fwT, 1)
            for k in range(KD):
                ins = pe.matmul(bank[1][:, 0:D], f_qT[:, k, :], f_wT[:, k, :], start=(k == 0), stop=(k == KD - 1))
            ins.then_inc(s_ffn, 1)

        @block.scalar
        def _(act):
            for dst, src in ((lat_w, ln_l_w), (lat_b, ln_l_b), (ctx_w, ln_c_w), (ctx_b, ln_c_b)):
                act.dma_start(dst[:, :], col(src), allow_slow_non_contiguous=True).then_inc(s_cols, 16)
            act.wait_ge(s_const, 2)
            act.activation(warm[:, :], neg_half[:, :], ACT.Exp)

            def store_cT(b, i):
                for k in range(KD):
                    ins = act.activation(cT_all[:, bass.ds(2 * i + b, 1), k, :],
                                         tr_bank[b][:, k * P:(k + 1) * P].unsqueeze(1), ACT.Identity,
                                         bias=ctx_b[:, k:k + 1], scale=ctx_w[:, k:k + 1])
                ins.then_inc(s_cT, 1)

            def exps(g, c, first=False, transposed=None):
                if transposed is not None:
                    act.wait_ge(s_tr, transposed)
                act.wait_ge(s_scores, CH * g + c + 1)
                if not first:
                    act.wait_ge(s_psplit, CH * (g - 1) + c + 1)
                act.activation(ex[c][:, :], sc_bank[c][:, :], ACT.Exp, scale=SCALE).then_inc(s_exp, 1)

            act.wait_ge(s_cols, COLS)
            act.wait_ge(s_latTp, 1)
            for k in range(KD):
                act.activation(latT[:, k, :], bank[4][:, k * P:(k + 1) * P], ACT.Identity, bias=lat_b[:, k:k + 1],
                               scale=lat_w[:, k:k + 1]).then_inc(s_latT, 1)

            for n in range(0, 4, 2):
                act.wait_ge(s_wkTp, n + 1)
                if n:
                    act.wait_ge(s_wkT, n)
                act.copy(wkT[:, 2 * n:2 * n + 2, :], bank[n][:, :].rearrange("p (m d) -> p m d", m=2))\
                   .then_inc(s_wkT, 1)
            act.wait_ge(s_const, 3)
            for n in range(2):
                act.wait_ge(s_qTp, n + 1)
                act.copy(qTbd[0:DH, 4 * n:4 * n + 4, 0, :],
                         bank[4 + n][0:DH, :].rearrange("p (m q) -> p m q", m=4)).then_inc(s_qTtop, 1)
            for b in range(2):
                act.wait_ge(s_tr, b + 1)
                store_cT(b, 0)
            for n in range(8):
                mm, k = n // KD, n % KD
                act.wait_ge(s_qkp, n + 1)
                act.copy(qk_hi[:, k, mm * 512:(mm + 1) * 512], bank[n % 4][:, :]).then_inc(s_qkhi, 1)
            exps(0, 0, first=True)
            exps(0, 1, first=True)

            def pair(p, i):
                for b in range(2):
                    g = 2 * (p * PAIRS + i) + b
                    static = isinstance(i, int)
                    ended = static and p == PASSES - 1
                    store = p == 0 and not (static and i == PAIRS - 1)
                    if not (ended and g + 1 >= ALL):
                        exps(g + 1, 0, transposed=g + 3 if store else None)
                    if store:
                        store_cT(b, i + 1)
                    if static and i == PAIRS - 1 and b == 1:
                        act.wait_ge(s_pv, CH * g + 1)
                        for k in range(KD):
                            act.copy(sums[:, k, p * HP * P:p * HP * P + CW], acc[k][0][:, :]).then_inc(s_save[0], 1)
                    if not (ended and g + 1 >= ALL):
                        exps(g + 1, 1)

            passes(act, pair)

            for n in range(4):
                half, kd = n // 2, n % 2
                act.wait_ge(s_wvp, n + 1)
                act.copy(wvE[:, kd, 8 * half:8 * half + 8, 0:DH],
                         bank[4 + n][:, :].rearrange("p (h d) -> p h d", h=8)).then_inc(s_wvE, 1)

            def effective_weights(n):
                act.wait_ge(s_awp[n], 1)
                act.copy(awE[n][:, :, :], bank[AW_BANK[n]][:, :].rearrange("p (k d) -> p k d", k=KD))\
                   .then_inc(s_awE[n], 1)

            def self_exp(n):
                act.wait_ge(s_ashift, n + 1)
                act.activation(a_p[:, 4 * n:4 * n + 4, :], a_p[:, 4 * n:4 * n + 4, :], ACT.Exp,
                               scale=AD ** -0.5).then_inc(s_aexp, 1)

            act.wait_ge(s_attTp, 1)
            act.copy(attT[:, 0:4, :], bank[4][:, :].rearrange("p (m q) -> p m q", m=4)).then_inc(s_attT0, 1)
            effective_weights(1)
            effective_weights(0)
            act.wait_ge(s_late, LATE)
            act.wait_ge(s_akp, 1)
            act.activation(a_k1[:, :], bank[1][:, P:2 * P], ACT.Identity, bias=abk_col[:, 1:2], scale=1.0)\
               .then_inc(s_ak1, 1)
            act.wait_ge(s_aqp, 1)
            for m in range(KD):
                ins = act.activation(aqT[:, m, :], bank[2][:, m * P:(m + 1) * P], ACT.Identity,
                                     bias=abq_col[:, m:m + 1], scale=1.0)
            ins.then_inc(s_aqT, 1)
            self_exp(0)
            self_exp(1)
            effective_weights(2)
            self_exp(2)
            self_exp(3)
            act.wait_ge(s_avp, 1)
            act.wait_ge(s_const, 6)
            act.copy(av[:, :, 0:AD], bank[5][:, 0:D].rearrange("p (h d) -> p h d", h=AH)).then_inc(s_av, 1)
            act.wait_ge(s_apTp, 3)
            act.copy(a_pT[:, 8:12, :], bank[2][:, :].rearrange("p (h t) -> p h t", h=4)).then_inc(s_apT2, 1)
            effective_weights(3)
            act.wait_ge(s_fwTp, 1)
            act.copy(f_wT[:, :, :], bank[7][:, 0:D].bitcast(BF16).rearrange("p (k d) -> p k d", k=KD)).then_inc(s_fwT, 1)
            act.wait_ge(s_fqTp, 1)
            act.copy(f_qT[:, :, :], bank[0][:, 0:P].bitcast(BF16).rearrange("p (k q) -> p k q", k=KD)).then_inc(s_fqT, 1)
            act.wait_ge(s_y, 1)
            act.dma_start(out_rows, y[:, :]).then_inc(s_out, 16)

        @block.vector
        def _(dve):
            count = [0]

            def link(ins):
                count[0] += 1
                ins.then_inc(s_dstep, 1)
                dve.wait_ge(s_dstep, count[0])

            nvar = [0]

            def normalise(dst, src):
                nvar[0] += 1
                link(dve.bn_stats(stats[:, :], src[:, :]))
                link(dve.bn_aggr(mv[:, :], stats[:, :]))
                dve.tensor_scalar(veps[:, :], mv[:, 1:2], EPS, None, ALU.add).then_inc(s_var, 1)
                dve.wait_ge(s_rstd, nvar[0])
                return dve.tensor_scalar(dst[:, :], src[:, :], mv[:, 0:1], rstd[:, 0:1], ALU.subtract, ALU.mult)

            dve.wait_ge(s_x, 16)
            link(normalise(xn, x_sb))
            normalise(lat, xn).then_inc(s_latn, 1)

            def tile_stats(tiles_of_b, b):
                dve.wait_ge(s_tile[b], 16 * tiles_of_b)
                dve.bn_stats(c_stats[b][:, :], x_tile[b][:, :]).then_inc(s_cst, 1)

            def tile_aggr(g, b, waited=False):
                if not waited:
                    dve.wait_ge(s_cst, g + 1)
                dve.bn_aggr(c_mv[b][:, :], c_stats[b][:, :]).then_inc(s_cag, 1)

            def tile_veps(g, b):
                dve.wait_ge(s_cag, g + 1)
                dve.tensor_scalar(c_veps[b][:, :], c_mv[b][:, 1:2], EPS, None, ALU.add).then_inc(s_cvar, 1)

            def tile_z(g, b, first=False, transposed=None):
                dve.wait_ge(s_crstd, g + 1)
                if not first:
                    if transposed is not None:
                        dve.wait_ge(s_tr, transposed)
                    dve.wait_ge(s_zsplit, g - 1)
                dve.tensor_scalar(z[b][:, :], x_tile[b][:, :], c_mv[b][:, 0:1], c_rstd[b][:, 0:1], ALU.subtract,
                                  ALU.mult).then_inc(s_z, 1)

            def split_cT_hi(p, g, b, i, first=False):
                if not first:
                    dve.wait_ge(s_scores, CH * (g - 1))
                if p == 0:
                    dve.wait_ge(s_cT, g + 1)
                dve.tensor_scalar(cT_hi[b][:, :, :].unsqueeze(1), cT_all[:, bass.ds(2 * i + b, 1), :, :], 1.0, None,
                                  ALU.mult).then_inc(s_cth, 1)

            def split_cT_lo(g, b, i):
                dve.wait_ge(s_cth, g + 1)
                dve.tensor_tensor(cT_lo[b][:, :, :].unsqueeze(1), cT_all[:, bass.ds(2 * i + b, 1), :, :],
                                  cT_hi[b][:, :, :].unsqueeze(1).bitcast(F32), ALU.subtract).then_inc(s_cTsplit, 1)

            def clip_hi(g, b, c, first=False, stats_of=None):
                dve.wait_ge(s_exp, CH * g + c + 1)
                if not first:
                    dve.wait_ge(s_pv, CH * (g - 2) + c + 1)
                dve.tensor_scalar(p_hi[b][c][:, :], ex[c][:, :], EXP_LO, EXP_HI, ALU.max, ALU.min).then_inc(s_phi, 1)
                if stats_of is not None:
                    dve.wait_ge(s_cst, stats_of + 1)
                dve.tensor_scalar(ex[c][:, :], ex[c][:, :], EXP_LO, EXP_HI, ALU.max, ALU.min).then_inc(s_clip, 1)

            def split_p_lo(g, b, c):
                dve.wait_ge(s_phi, CH * g + c + 1)
                dve.wait_ge(s_clip, CH * g + c + 1)
                dve.tensor_tensor(p_lo[b][c][:, :], ex[c][:, :], p_hi[b][c][:, :].bitcast(F32), ALU.subtract)\
                   .then_inc(s_psplit, 1)

            for g in range(2):
                tile_stats(1, g)
                tile_aggr(g, g)
                tile_veps(g, g)
            for g in range(2):
                tile_z(g, g, first=True)
            for n in range(1, 4, 2):
                dve.wait_ge(s_wkTp, n + 1)
                dve.wait_ge(s_wkT, n)
                dve.tensor_copy(wkT[:, 2 * n:2 * n + 2, :], bank[n][:, :].rearrange("p (m d) -> p m d", m=2))\
                   .then_inc(s_wkT, 1)

            dve.wait_ge(s_const, 3)
            for n in range(2):
                dve.wait_ge(s_qTp, n + 1)
                dve.wait_ge(s_qTtop, n + 1)
                dve.tensor_copy(qTbd[DH:P, 4 * n:4 * n + 4, 1, :],
                                bank[4 + n][DH:P, :].rearrange("p (m q) -> p m q", m=4)).then_inc(s_qTbot, 1)
            for g in range(2):
                split_cT_hi(0, g, g, 0, first=True)
                split_cT_lo(g, g, 0)
            tile_stats(2, 0)
            tile_aggr(2, 0)
            tile_veps(2, 0)
            for n in range(8):
                if n == 4:
                    tile_z(2, 0, transposed=1)
                mm, k = n // KD, n % KD
                cols = slice(mm * 512, (mm + 1) * 512)
                dve.wait_ge(s_qkp, n + 1)
                dve.wait_ge(s_qkhi, n + 1)
                dve.tensor_tensor(qk_lo[:, k, cols], bank[n % 4][:, :], qk_hi[:, k, cols].bitcast(F32), ALU.subtract)\
                   .then_inc(s_qklo, 1)
            for c in range(CH):
                clip_hi(0, 0, c, first=True)
                split_p_lo(0, 0, c)

            def pair(p, i):
                for b in range(2):
                    gp = p * PAIRS + i
                    g = 2 * gp + b
                    static = isinstance(i, int)
                    ended = static and p == PASSES - 1
                    more1 = not (ended and g + 1 >= ALL)
                    more2 = not (ended and g + 2 >= ALL)
                    more3 = not (ended and g + 3 >= ALL)
                    start = static and g == 0
                    over = static and i == PAIRS - 1
                    if more3:
                        tile_stats(gp + 2 + b, 1 - b)
                    if static and i == 0 and b == 0 and p > 0:
                        save_chunk1(p - 1)
                    if more1:
                        clip_hi(g + 1, 1 - b, 0, first=start, stats_of=g + 3 if more3 else None)
                    if more3:
                        tile_aggr(g + 3, 1 - b, waited=True)
                    if more1:
                        split_p_lo(g + 1, 1 - b, 0)
                    if more3:
                        tile_veps(g + 3, 1 - b)
                    if more2:
                        ni = 0 if over else i + 1
                        split_cT_hi(1 if over else p, g + 2, b, ni)
                        split_cT_lo(g + 2, b, ni)
                    if more3:
                        tile_z(g + 3, 1 - b, transposed=None if p else min(g + 2, TILES) if static else g + 2)
                    if more1:
                        clip_hi(g + 1, 1 - b, 1, first=start)
                        split_p_lo(g + 1, 1 - b, 1)
                    if static and p == PASSES - 1 and i == PAIRS - 3 and b == 0:
                        fold_weights()

            def fold_weights():
                dve.wait_ge(s_const, 7)
                dve.wait_ge(s_cols, COLS)
                dve.tensor_copy(identb[:, :], ident[:, :])
                link(dve.scalar_tensor_tensor(neg_w_last[:, :], ctx_w[:, 1:2], -1.0, last_row[:, :], ALU.mult, ALU.mult))
                dve.tensor_scalar(foldT[:, 0, 0:P], ident[:, :], ctx_w[:, 0:1], None, ALU.mult)
                dve.tensor_scalar(foldT[:, 1, 0:P], ident[:, :], 0.0, neg_w_last[:, 0:1], ALU.mult, ALU.add)
                link(dve.tensor_scalar(foldT[:, 1, P:D], ident[:, :], ctx_w[:, 1:2], neg_w_last[:, 0:1], ALU.mult, ALU.add))
                for k in range(KD):
                    ins = dve.tensor_copy(foldT[:, k, D - 1:D], ctx_b[:, k:k + 1])
                ins.then_inc(s_foldT, 1)

            def save_chunk1(p):
                dve.wait_ge(s_pv, CH * TILES * (p + 1))
                for k in range(KD):
                    dve.tensor_copy(sums[:, k, p * HP * P + CW:(p + 1) * HP * P], acc[k][1][:, :])\
                       .then_inc(s_save[1], 1)

            passes(dve, pair)

            dve.memset(wvE[:, 0, :, DH:VW], 0.0)
            dve.tensor_copy(wvE[:, 1, :, DH:VW], last_row[:, 0:1].unsqueeze(1).to_broadcast([P, H, 1])).then_inc(s_wvden, 1)
            save_chunk1(PASSES - 1)

            def fp8_weights():
                link(dve.tensor_copy(f_u[:, :, :], f_bytes[:, :, :]))
                dve.tensor_scalar(f_mag[:, :, :], f_u[:, :, :], 0x7F, 7, ALU.bitwise_and, ALU.logical_shift_left)
                link(dve.tensor_scalar(f_sgn[:, :, :], f_u[:, :, :], 0x80, 8, ALU.bitwise_and, ALU.logical_shift_left))
                link(dve.tensor_tensor(f_h[:, :, :], f_mag[:, :, :], f_sgn[:, :, :], ALU.bitwise_or))
                dve.tensor_scalar(f_w[:, :, :], f_h[:, :, :].bitcast(FP16), 256.0, None, ALU.mult).then_inc(s_fw, 1)

            def per_head(t, n, w):
                return t.unsqueeze(2).to_broadcast([P, n, w])

            dve.wait_ge(s_late, LATE)
            dve.tensor_scalar(aa_all, aa_all, LORA_SCALE, None, ALU.mult).then_inc(s_lora, 1)
            fp8_weights()
            banks_of = [range(j, min(j + HB, H)) for j in range(0, H, HB)]
            for j, hs in enumerate(banks_of):
                o = bank[j][:, 0:len(hs) * VW].rearrange("p (h v) -> p h v", v=VW)
                dve.wait_ge(s_heads, j + 1)
                dve.reciprocal(recip[:, hs[0]:hs[-1] + 1].unsqueeze(2), o[:, :, DH:VW]).then_inc(s_recip, 1)
                dve.wait_ge(s_recip, j + 1)
                dve.tensor_tensor(att[:, hs[0]:hs[-1] + 1, :], o[:, :, 0:DH],
                                  per_head(recip[:, hs[0]:hs[-1] + 1], len(hs), DH), ALU.mult).then_inc(s_att, 1)
            dve.wait_ge(s_attTp, 2)
            dve.tensor_copy(attT[:, 4:8, :], bank[5][:, :].rearrange("p (m q) -> p m q", m=4)).then_inc(s_attT1, 1)
            dve.wait_ge(s_xattn, 1)
            link(dve.tensor_tensor(x1[:, :], x_sb[:, :], bank[0][:, 0:D], ALU.add))
            normalise(hn, x1).then_inc(s_hn, 1)
            dve.wait_ge(s_hTp, 1)
            dve.tensor_copy(hT[:, :, :], bank[1][:, 0:D].rearrange("p (k q) -> p k q", k=KD)).then_inc(s_hT, 1)
            dve.wait_ge(s_akp, 1)
            dve.scalar_tensor_tensor(akT[:, 0, :, :], bank[3][:, 0:P].unsqueeze(1).to_broadcast([P, HT, P]),
                                     abk_col[:, 0:1], per_head(head_mask[:, :], HT, P), ALU.add, ALU.mult)\
               .then_inc(s_akT[0], 1)
            for n in range(4):
                s_view = bank[4 + n][:, :].rearrange("p (h t) -> p h t", h=4)
                dve.wait_ge(s_ascore, n + 1)
                dve.tensor_reduce(a_max[:, 4 * n:4 * n + 4], s_view, AX_X, ALU.max).then_inc(s_amax, 1)
                dve.wait_ge(s_amax, n + 1)
                dve.tensor_tensor(a_p[:, 4 * n:4 * n + 4, :], s_view, per_head(a_max[:, 4 * n:4 * n + 4], 4, P),
                                  ALU.subtract).then_inc(s_ashift, 1)
            for n in (0, 1, 3):
                dve.wait_ge(s_apTp, n + 1)
                dve.tensor_copy(a_pT[:, 4 * n:4 * n + 4, :], bank[n][:, :].rearrange("p (h t) -> p h t", h=4))\
                   .then_inc(s_apT, 1)
            dve.wait_ge(s_apv, 1)
            o = bank[4][:, 0:AH * (AD + 1)].rearrange("p (h v) -> p h v", v=AD + 1)
            link(dve.reciprocal(a_recip[:, :].unsqueeze(2), o[:, :, AD:AD + 1]))
            dve.tensor_tensor(ao[:, :, :], o[:, :, 0:AD], per_head(a_recip[:, :], AH, AD), ALU.mult).then_inc(s_ao, 1)
            dve.wait_ge(s_aoTp, 1)
            dve.tensor_copy(aoT[:, :, :], bank[5][:, 0:D].rearrange("p (k q) -> p k q", k=KD)).then_inc(s_aoT, 1)
            dve.wait_ge(s_attn, 1)
            link(dve.tensor_tensor(x2[:, :], x1[:, :], bank[6][:, 0:D], ALU.add))
            link(normalise(fn, x2))
            link(dve.tensor_reduce(amax[:, :], fn[:, :], AX_X, ALU.max, apply_absolute_value=True))
            link(dve.tensor_scalar(f_xs[:, :], amax[:, :], 1e-12, 1.0 / FP8_MAX, ALU.max, ALU.mult))
            link(dve.reciprocal(f_inv[:, :], f_xs[:, :]))
            link(dve.tensor_scalar(fv[:, :], fn[:, :], f_inv[:, 0:1], None, ALU.mult))
            link(dve.tensor_scalar(f_pow[:, :].bitcast(I32), fv[:, :].bitcast(I32), 0x7F800000, None, ALU.bitwise_and))
            link(dve.tensor_scalar(f_magic[:, :], f_pow[:, :], 2.0 ** -6, 1.5 * 2.0 ** 20, ALU.max, ALU.mult))
            link(dve.tensor_tensor(f_sum[:, :], fv[:, :], f_magic[:, :], ALU.add))
            dve.tensor_tensor(f_q[:, :], f_sum[:, :], f_magic[:, :], ALU.subtract).then_inc(s_fq, 1)
            dve.tensor_tensor(f_row_scale[:, :], f_xs[:, :], f_ws[:, :], ALU.mult)
            link(dve.tensor_tensor(x2b[:, :], x2[:, :], f_b[:, :], ALU.add))
            dve.wait_ge(s_ffn, 1)
            dve.scalar_tensor_tensor(y[:, :], bank[1][:, 0:D], f_row_scale[:, 0:1], x2b[:, :], ALU.mult, ALU.add)\
               .then_inc(s_y, 1)


_INS = ['x', 'ctx_1024', 'L0_xattn_ln_l_w', 'L0_xattn_ln_l_b', 'L0_xattn_ln_c_w', 'L0_xattn_ln_c_b', 'L0_xattn_Wq',
        'L0_xattn_Wkv', 'L0_xattn_Wo', 'L0_xattn_bo',
        'L0_attn_Wq', 'L0_attn_bq', 'L0_attn_Aq', 'L0_attn_Bq', 'L0_attn_Wk', 'L0_attn_bk', 'L0_attn_Ak', 'L0_attn_Bk',
        'L0_attn_Wv', 'L0_attn_bv', 'L0_attn_Av', 'L0_attn_Bv', 'L0_attn_Wo', 'L0_attn_bo', 'L0_attn_Ao', 'L0_attn_Bo',
        'L0_ffn_weight', 'L0_ffn_weight_scale', 'L0_ffn_bias']
_OUTS = [((1, 128, 256), 'float32')]


def kernel(**inputs):
    import concourse.bacc as _bacc
    from concourse.bass_utils import run_bass_kernel_spmd as _run

    nc = _bacc.Bacc("TRN2", target_bir_lowering=False, num_devices=1)
    arrays, args = {}, []
    for name in _INS:
        a = np.ascontiguousarray(inputs[name])
        arrays[f"in_{name}_dram"] = a
        args.append(nc.dram_tensor(f"in_{name}_dram", a.shape, mybir.dt.from_np(a.dtype), kind="ExternalInput").ap())
    for i, (shape, dtype) in enumerate(_OUTS):
        dt = mybir.dt.from_np(np.dtype(dtype))
        args.append(nc.dram_tensor(f"out_{i}_dram", shape, dt, kind="ExternalOutput").ap())
    perceiver_layer(nc, *args)
    r = _run(nc, [arrays], core_ids=[0])
    return r.results[0]["out_0_dram"]
```
